# Optimizing a Trainium2 kernel written in Bass

```python
import numpy as np
import jax
import jax.numpy as jnp

def _softmax(x, axis=-1):
    return jax.nn.softmax(x, axis=axis)

def _gelu(x):
    return jax.nn.gelu(x, approximate=True)

def _silu(x):
    return jax.nn.silu(x)

def _sigmoid(x):
    return jax.nn.sigmoid(x)

def _layernorm(x, axis=-1, eps=1e-05):
    m = jnp.mean(x, axis=axis, keepdims=True)
    v = jnp.var(x, axis=axis, keepdims=True)
    return (x - m) / jnp.sqrt(v + eps)

def _scatter_add(tgt, idx, src, axis=0):
    return tgt.at[idx].add(src)

def _segment_sum(src, seg, n):
    return jax.ops.segment_sum(src, seg, n)
kernel_name = 'mk_recurrent_d1_jaxref_r4_aa4fe6'

def setup_inputs(seed: int=0):
    np.random.seed(seed)
    _w = jnp.asarray

    def _L0_attn_setup():
        import jax, jax.numpy as jnp
        import numpy as np
        D_MODEL = 512
        N_HEADS = 16
        SEQ_LEN = 512
        BATCH = 2
        BIAS_MAX = 8.0

        def alibi_bias(n_heads, seq_len, dtype):
            pos = jnp.arange(1 - seq_len, 1, dtype=dtype)
            m = jnp.arange(1, n_heads + 1, dtype=dtype) * (BIAS_MAX / n_heads)
            slopes = 1.0 / 2.0 ** m
            return pos[None, :] * slopes[:, None]
        key = jax.random.key(seed)
        k1, k2, k3 = jax.random.split(key, 3)
        s = 1.0 / np.sqrt(D_MODEL)
        x = jax.random.normal(k1, (BATCH, SEQ_LEN, D_MODEL), dtype=jnp.float32)
        Wqkv = jax.random.normal(k2, (3 * D_MODEL, D_MODEL), dtype=jnp.float32) * s
        b_qkv = jnp.zeros((3 * D_MODEL,), dtype=jnp.float32)
        Wout = jax.random.normal(k3, (D_MODEL, D_MODEL), dtype=jnp.float32) * s
        b_out = jnp.zeros((D_MODEL,), dtype=jnp.float32)
        return {'x': x, 'Wqkv': Wqkv, 'b_qkv': b_qkv, 'Wout': Wout, 'b_out': b_out}
    _L0_attn_in = _L0_attn_setup()

    def _L0_ffn_setup():
        import jax, jax.numpy as jnp
        import numpy as np
        DIM = 512
        HIDDEN = 2048
        NUM_EXPERTS = 2
        BATCH, SEQ = (4, 256)
        key = jax.random.key(seed)
        k1, k2, k3, k4 = jax.random.split(key, 4)
        x = jax.random.normal(k1, (BATCH, SEQ, DIM), dtype=jnp.float32)
        w_router = jax.random.normal(k2, (NUM_EXPERTS, DIM), dtype=jnp.float32) * (1.0 / np.sqrt(DIM))
        w_fc = jax.random.normal(k3, (NUM_EXPERTS, HIDDEN, DIM), dtype=jnp.float32) * (1.0 / np.sqrt(DIM))
        w_proj = jax.random.normal(k4, (NUM_EXPERTS, DIM, HIDDEN), dtype=jnp.float32) * (1.0 / np.sqrt(HIDDEN))
        return {'x': x, 'w_router': w_router, 'w_fc': w_fc, 'w_proj': w_proj}
    _L0_ffn_in = _L0_ffn_setup()
    _d = {'L0_attn_x': _L0_attn_in['x'], 'L0_attn_Wqkv': _L0_attn_in['Wqkv'], 'L0_attn_b_qkv': _L0_attn_in['b_qkv'], 'L0_attn_Wout': _L0_attn_in['Wout'], 'L0_attn_b_out': _L0_attn_in['b_out'], 'L0_ffn_w_router': _L0_ffn_in['w_router'], 'L0_ffn_w_fc': _L0_ffn_in['w_fc'], 'L0_ffn_w_proj': _L0_ffn_in['w_proj']}
    _x0 = _d['L0_attn_x']
    _d['L0_attn_x'] = jax.random.normal(jax.random.fold_in(jax.random.key(seed), 1), (8, 512, 512), dtype=_x0.dtype)
    del _x0
    return _d

def reference(L0_attn_x, L0_attn_Wqkv, L0_attn_b_qkv, L0_attn_Wout, L0_attn_b_out, L0_ffn_w_router, L0_ffn_w_fc, L0_ffn_w_proj):

    def _L0_attn_ref(x, Wqkv, b_qkv, Wout, b_out):
        import jax, jax.numpy as jnp
        import numpy as np
        D_MODEL = 512
        N_HEADS = 16
        SEQ_LEN = 512
        BATCH = 2
        BIAS_MAX = 8.0

        def alibi_bias(n_heads, seq_len, dtype):
            pos = jnp.arange(1 - seq_len, 1, dtype=dtype)
            m = jnp.arange(1, n_heads + 1, dtype=dtype) * (BIAS_MAX / n_heads)
            slopes = 1.0 / 2.0 ** m
            return pos[None, :] * slopes[:, None]
        B, S, D = x.shape
        H = N_HEADS
        hd = D // H
        scale = 1.0 / jnp.sqrt(jnp.asarray(hd, dtype=x.dtype))
        qkv = x @ Wqkv.T + b_qkv
        q, k, v = jnp.split(qkv, 3, axis=-1)
        q = q.reshape(B, S, H, hd)
        k = k.reshape(B, S, H, hd)
        v = v.reshape(B, S, H, hd)
        scores = jnp.einsum('bqhd,bkhd->bhqk', q, k) * scale
        bias = alibi_bias(H, S, x.dtype)
        scores = scores + bias[None, :, None, :]
        causal = jnp.tril(jnp.ones((S, S), dtype=bool))
        scores = jnp.where(causal[None, None, :, :], scores, jnp.asarray(-1000000000.0, dtype=x.dtype))
        p = jax.nn.softmax(scores, axis=-1)
        ctx = jnp.einsum('bhqk,bkhd->bqhd', p, v).reshape(B, S, D)
        return ctx @ Wout.T + b_out

    def _L0_ffn_ref(x, w_router, w_fc, w_proj):
        import jax, jax.numpy as jnp
        import numpy as np
        DIM = 512
        HIDDEN = 2048
        NUM_EXPERTS = 2
        BATCH, SEQ = (4, 256)
        bsz, seq, dim = x.shape
        num_experts = w_router.shape[0]
        x_flat = x.reshape(-1, dim)
        logits = x_flat @ w_router.T
        probs = jax.nn.softmax(logits, axis=-1)
        top_idx = jnp.argmax(probs, axis=-1)
        top_weight = jnp.take_along_axis(probs, top_idx[:, None], axis=1)[:, 0]
        h = jnp.einsum('nd,ehd->enh', x_flat, w_fc)
        a = jnp.square(jnp.where(h >= 0, h, 0.5 * h))
        expert_out = jnp.einsum('enh,edh->end', a, w_proj)
        mask = (top_idx[None, :] == jnp.arange(num_experts)[:, None]).astype(x.dtype)
        out = jnp.einsum('end,en->nd', expert_out, mask * top_weight[None, :])
        return out.reshape(bsz, seq, dim)
    x = L0_attn_x
    xn = _layernorm(x, axis=-1)
    s = _L0_attn_ref(xn, L0_attn_Wqkv, L0_attn_b_qkv, L0_attn_Wout, L0_attn_b_out)
    g = _silu(_L0_ffn_ref(xn, L0_ffn_w_router, L0_ffn_w_fc, L0_ffn_w_proj))
    x = x + s * g
    return x

_drawn_inputs = setup_inputs


def setup_inputs(seed=0):
    import zlib

    import numpy as np

    out = dict(_drawn_inputs(seed))
    spreads = {'L0_attn_b_qkv': (0.0, 0.1), 'L0_attn_b_out': (0.0, 0.1)}
    factors = {}
    for name, (base, spread) in spreads.items():
        noise = np.random.default_rng([zlib.crc32(name.encode()), seed]).standard_normal(out[name].shape)
        drawn = base * np.exp(spread * noise) if base else spread * noise
        out[name] = jnp.asarray(drawn.astype(out[name].dtype))
    for name, factor in factors.items():
        out[name] = (out[name] * factor).astype(out[name].dtype)
    return out
```

```python
import concourse.bass as bass
from concourse import mybir
from concourse.alu_op_type import AluOpType as ALU
from contextlib import ExitStack
import numpy as np

P = 128
B, S, D = 8, 512, 512
H, HD = 16, 32
TOK = B * S
KC = D // P
QB = S // P
HG = P // HD
NG = H // HG
NU = B * NG
E, HID = 2, 2048
HC = HID // 512
SLOTS = TOK // P + 1
MROW = 8
MASK = -float(2 ** 40)
OOB = 8192

ROWOFF = [P * i * (i + 1) // 2 for i in range(QB)]
CAUSAL = P * QB * (QB + 1) // 2
SEG = {0: 0, 1: 512, 3: 896, 2: 1024}
TJOBS = [[0], [1, 3], [2]]

F32, F16, I32 = mybir.dt.float32, mybir.dt.float16, mybir.dt.int32
ACT = mybir.ActivationFunctionType
AX = mybir.AxisListType
RMAX = bass.bass_isa.ReduceOp.max

C_ID, C_LT, C_BASE, C_F, C_TOK, C_NSL, C_SLOT = 0, 128, 256, 768, 772, 776, 792
C_N = C_SLOT + SLOTS
(X_SWQ, X_SWO, X_SWR, X_CK, X_CC, X_CS, X_CR, X_PA, X_PM, X_PAO, X_PAR, X_RPM, X_T0, X_T1,
 X_S1, X_S2, X_CY, X_PA1, X_PA2, X_N) = range(20)


def constants():
    c = np.zeros((P, C_N), np.float32)
    p = np.arange(P)
    c[:, C_ID:C_ID + P] = np.eye(P)
    c[:, C_LT:C_LT + P] = p[:, None] < p[None, :]
    k = np.arange(S)
    c[:, C_BASE:C_BASE + S] = k[None, :] - (S - 1)
    c[:, C_BASE + S - P:C_BASE + S] += np.where(p[None, :] > p[:, None], MASK, 0.0)
    slope = 2.0 ** (-(np.arange(H) + 1) * 8.0 / H)
    for g in range(NG):
        c[:, C_F + g] = (HD ** -0.5) / slope[g * HG + p // HD]
    for i in range(QB):
        c[:, C_TOK + i] = i * P + p
    c[:, C_NSL:C_NSL + H] = -slope[None, :]
    c[:, C_SLOT:C_SLOT + SLOTS] = P * np.arange(SLOTS)[None, :]
    return c


def wait(eng, sem, value, apart=None):
    if isinstance(value, int) and value <= 0:
        return
    eng.wait_ge(sem, value)
    if apart is not None and not isinstance(value, int):
        eng.sem_inc(apart, 1)


def within(n, lo, hi):
    return not isinstance(n, int) or lo <= n < hi


def batches(eng, iteration):
    iteration(-1, 1)
    iteration(0, 0)
    with eng.Fori(0, (B - 2) // 2) as it:
        iteration(it * 2 + 1, 1)
        iteration(it * 2 + 2, 0)
    iteration(B - 1, 1)
    iteration(B, 0)


NJOB = 21
ABANKS = 3


def job_exists(b, pos):
    if not isinstance(b, int):
        return True
    if pos in (0, 1, 6, 7):
        return 0 <= b < B
    if 2 <= pos <= 5:
        return 1 <= b <= B
    return -1 <= b <= B - 2


def attention_block(nc, io, sc, conf, esum):
    with ExitStack() as ctx:
        sb = lambda n, s, d: ctx.enter_context(nc.sbuf_tensor(n, s, d))
        sem = lambda n: ctx.enter_context(nc.semaphore(n))
        wqkv = sb("wqkv", [P, KC, 2, 3 * D], F16)
        wout = sb("wout", [P, NG, 2, D], F16)
        wr = sb("wr", [P, KC, 2, E], F16)
        wr_f = sb("wr_f", [P, KC * E], F32)
        bqk = sb("bqk", [P, 3 * NG], F32)
        bqs = sb("bqs", [P, 3 * NG], F32)
        cq = sb("cq", [P, NG], F32)
        nsl = sb("nsl", [P, H], F32)
        base = sb("base", [P, S], F32)
        bout = sb("bout", [P, D], F32)
        lt16 = sb("lt16", [P, P], F16)
        ones16 = sb("ones16", [P, P], F16)
        tid = sb("tid", [P, QB], F32)
        am = sb("am", [P, 8], F32)
        amr = sb("amr", [P, 8], F32)
        fam = sb("fam", [P, 4], F32)
        xin = sb("xin", [P, QB, D], F32)
        xn = sb("xn", [P, QB, D], F32)
        stat = sb("stat", [P, QB, 6], F32)
        mv = sb("mv", [P, QB, 2], F32)
        veps = sb("veps", [P, QB], F32)
        half = sb("half", [P, QB], F32)
        rstd = sb("rstd", [P, 2, QB], F32)
        xT = sb("xT", [P, 2, 2, KC, S], F16)
        stage = sb("stage", [P, 2, S], F32)
        pre = sb("pre", [P, 2, 2, S], F16)
        qs = sb("qs", [P, 2, HG, S], F16)
        ks = sb("ks", [P, 2, HG, S], F16)
        v = sb("v", [P, 2, 2, QB, D], F16)
        pr = sb("pr", [P, HG, CAUSAL], F32)
        mn = sb("mn", [P, HG * QB], F32)
        den = sb("den", [P, HG * QB], F32)
        rden = sb("rden", [P, HG * QB], F32)
        pt = sb("pt", [P, 2, 2, HG, CAUSAL], F16)
        cf = sb("cf", [P, S], F32)
        cx = sb("cx", [P, NG, 2, S], F16)
        so = sb("so", [P, QB, D], F32)
        wst = sb("wst", [P, 2048], F32)
        lg = sb("lg", [P, QB, E], F32)
        dl = sb("dl", [P, QB], F32)
        nd = sb("nd", [P, QB], F32)
        ex = sb("ex", [P, QB], F32)
        e16 = sb("e16", [P, QB + 1], F16)
        epre = sb("epre", [P, QB + 1], F16)
        ef = sb("ef", [P, QB + 1], F32)
        rk = sb("rk", [P, QB + 1], F32)
        t0 = sb("t0", [P, QB], F32)
        t1 = sb("t1", [P, QB], F32)
        pos = sb("pos", [P, QB], I32)
        meta = sb("meta", [P, QB, MROW], F32)

        psA = [ctx.enter_context(nc.psum_tensor(f"psA{i}", [P, 512], F32)) for i in range(ABANKS)]
        psS = [ctx.enter_context(nc.psum_tensor(f"psS{i}", [P, 512], F32)) for i in range(2)]
        psT = [ctx.enter_context(nc.psum_tensor(f"psT{i}", [P, 512], F32)) for i in range(2)]
        psC = ctx.enter_context(nc.psum_tensor("psC", [P, 512], F32))

        names = ("const_in w_in wr_in absmax allmax scales w_split_hi w_split_lo setup consts_made "
                 "ln_stats rstd_ready xn_ready xT_done xT_hi xT_lo V_done V_hi V_lo "
                 "qk_done qk_staged qk_hi qk_lo S_done ttr_done exp_done rden_done norm_done "
                 "T_done T_hi T_lo PV_done ctx_staged ctx_hi ctx_lo O_done O_evac "
                 "R_done R2_done rank_read e_ready nd_ready rexp_done meta_ready wmax_in wmax_done "
                 "apart_dve apart_sp apart_pool dve_link wm_link pool_link meta_out").split()
        s = {n: sem(n) for n in names}
        x_in = [sem(f"x_in{i}") for i in range(QB)]
        s_out = [sem(f"s_out{i}") for i in range(QB)]
        stored = [sem("q_stored"), sem("k_stored")]
        stacked = [[sem(f"{n}_stacked{p}") for p in range(2)] for n in "qk"]

        wflat = pt[:, :, :, :, :].rearrange("p a b h n -> p (a b h n)").bitcast(F32)
        wq_f = wflat[:, 0:KC * 3 * D]
        wo_f = wflat[:, KC * 3 * D:KC * 3 * D + NG * D]

        def bankof(g, w):
            return ({2: 0, 3: 6, 0: 12, 1: 17}[g] + w) % ABANKS

        block = ctx.enter_context(nc.Block())

        @block.sync
        def _(sp):
            for i in range(QB):
                sp.sem_inc(s_out[i], 16)
            sp.dma_start(conf[:], io["const"]).then_inc(s["const_in"], 16)
            for i in range(QB):
                sp.dma_start(xin[:, i, :], io["x"][i * P:(i + 1) * P, :]).then_inc(x_in[i], 16)
            sp.dma_start(wq_f, io["wqkv"]).then_inc(s["w_in"], 16)
            sp.dma_start(wo_f, io["wout"]).then_inc(s["w_in"], 16)
            sp.dma_start(wr_f[:], io["wr"]).then_inc(s["wr_in"], 16)
            sp.dma_start(bqk[:], io["bqkv"]).then_inc(s["wr_in"], 16)
            sp.dma_start(bout[:], io["bout"]).then_inc(s["wr_in"], 16)

            def stack(b, g):
                u = b * NG + g
                if not within(u, 0, NU):
                    return
                par = g % 2
                for w, dst, parts in ((0, qs, (0, 1, 0, 1)), (1, ks, (0, 0, 1, 1))):
                    wait(sp, s["qk_hi"], u * 2 + 1 + w, s["apart_sp"])
                    wait(sp, s["qk_lo"], u * 2 + 1 + w, s["apart_sp"])
                    wait(sp, stacked[w][par], (b * 2 + g // 2) * 64, s["apart_sp"])
                    sp.dma_start(io["qk"][w, par].rearrange("a p n -> p a n"),
                                 pre[:, w, :, :]).then_inc(stored[w], 16)
                    wait(sp, stored[w], (u + 1) * 16, s["apart_sp"])
                    wait(sp, s["S_done"], (u - 1) * 16, s["apart_sp"])
                    for r in range(4):
                        sp.dma_start(dst[r * HD:(r + 1) * HD, par, :, :],
                                     io["qk"][w, par, parts[r]].rearrange("(j d) n -> d j n", j=HG)
                                     ).then_inc(stacked[w][par], 16)

            def iteration(b, odd):
                if within(b, 0, B - 1):
                    for i in range(QB):
                        wait(sp, s["xn_ready"], b * QB + i + 1, s["apart_sp"])
                        sp.dma_start(xin[:, i, :], io["x"][bass.ds((b + 1) * S + i * P, P), :]
                                     ).then_inc(x_in[i], 16)
                if within(b, 0, B):
                    wait(sp, s["wmax_done"], b * 2, s["apart_sp"])
                    sp.dma_start(wst[:], io["wf"][bass.ds(b * 2, 1)].rearrange("o p n -> (o p) n")
                                 ).then_inc(s["wmax_in"], 16)
                    stack(b, 2)
                if within(b, 1, B + 1):
                    for i in range(QB):
                        wait(sp, s["O_evac"], (b - 1) * QB + i + 1, s["apart_sp"])
                        sp.dma_start(io["s"][bass.ds((b - 1) * S + i * P, P), :], so[:, i, :]
                                     ).then_inc(s_out[i], 16)
                if within(b, 0, B):
                    stack(b, 3)
                    wait(sp, s["wmax_done"], b * 2 + 1, s["apart_sp"])
                    sp.dma_start(wst[:], io["wf"][bass.ds(b * 2 + 1, 1)].rearrange("o p n -> (o p) n")
                                 ).then_inc(s["wmax_in"], 16)
                if within(b, -1, B - 1):
                    stack(b + 1, 0)
                    stack(b + 1, 1)

            batches(sp, iteration)
            for i in range(QB):
                sp.wait_ge(s_out[i], 16 * (B + 1))

        @block.tensor
        def _(pe):
            def bank(b, p):
                def release(b, p):
                    if p in (0, 1):
                        return s["qk_staged"], (b * 4 + 2) * 2 + 1 + p
                    if p in (6, 7):
                        return s["qk_staged"], (b * 4 + 3) * 2 + 1 + p - 6
                    if p in (12, 13):
                        return s["qk_staged"], (b * 4 + 4) * 2 + 1 + p - 12
                    if p in (17, 18):
                        return s["qk_staged"], (b * 4 + 5) * 2 + 1 + p - 17
                    if 2 <= p <= 5:
                        return s["O_evac"], (b - 1) * QB + p - 1
                    if 8 <= p <= 11:
                        return s["xT_lo"], (b + 1) * QB + p - 7
                    if p == 15:
                        return s["rank_read"], b + 2
                    return s["V_lo"], (b + 1) * QB + {14: 1, 16: 2, 19: 3, 20: 4}[p]

                bb, q = b, p - ABANKS
                while True:
                    if q < 0:
                        bb, q = bb - 1, q + NJOB
                    if isinstance(bb, int) and bb < -1:
                        break
                    if job_exists(bb, q):
                        if p != 12:
                            wait(pe, *release(bb, q))
                        break
                    q -= ABANKS
                return psA[p % ABANKS]

            def qk(b, g, w, p, it_b):
                if not within(b, 0, B):
                    return
                par = xpar(b, it_b)
                if g == 0 and w == 0:
                    wait(pe, s["xT_hi"], (b + 1) * QB)
                    wait(pe, s["xT_lo"], (b + 1) * QB)
                ps = bank(it_b[0], p)
                col = w * D + g * P
                n = 0
                for a, x in ((0, 0), (0, 1), (1, 0)):
                    for kc in range(KC):
                        last = nc.tensor.matmul(ps[:], wqkv[:, kc, a, col:col + P], xT[:, par, x, kc, :],
                                                start=(n == 0), stop=(n == 3 * KC - 1))
                        n += 1
                last.then_inc(s["qk_done"], 1)

            def xpar(b, it_b):
                return it_b[1] if b is it_b[0] else 1 - it_b[1]

            def vproj(b, i, p, it_b):
                par = 1 - it_b[1]
                ps = bank(it_b[0], p)
                n = 0
                for x, a in ((0, 0), (1, 0), (0, 1)):
                    for kc in range(KC):
                        last = nc.tensor.matmul(ps[:], xT[:, par, x, kc, i * P:(i + 1) * P],
                                                wqkv[:, kc, a, 2 * D:3 * D],
                                                start=(n == 0), stop=(n == 3 * KC - 1))
                        n += 1
                last.then_inc(s["V_done"], 1)

            def router(p, it_b):
                par = 1 - it_b[1]
                ps = bank(it_b[0], p)
                for i in range(QB):
                    n = 0
                    for x, a in ((0, 0), (1, 0), (0, 1)):
                        for kc in range(KC):
                            last = nc.tensor.matmul(ps[:, i * E:(i + 1) * E],
                                                    xT[:, par, x, kc, i * P:(i + 1) * P],
                                                    wr[:, kc, a, :], start=(n == 0), stop=(n == 3 * KC - 1))
                            n += 1
                last.then_inc(s["R_done"], 1)

            def rank(b):
                ps = psA[15 % ABANKS]
                wait(pe, s["e_ready"], b + 1)
                nc.tensor.matmul(ps[:, 16:16 + QB + 1], lt16[:], e16[:], start=True, stop=False)
                nc.tensor.matmul(ps[:, 16:16 + QB + 1], ones16[:], epre[:], start=False, stop=True
                                 ).then_inc(s["R2_done"], 1)

            def transposes(b, i, p, it_b):
                ps = bank(it_b[0], p)
                wait(pe, s["xn_ready"], b * QB + i + 1)
                for kc in range(KC):
                    last = nc.tensor.transpose(ps[:, kc * P:(kc + 1) * P], xn[:, i, kc * P:(kc + 1) * P],
                                               conf[:, C_ID:C_ID + P])
                last.then_inc(s["xT_done"], 1)

            def oproj(b, i, p, it_b):
                ps = bank(it_b[0], p)
                if i == 0:
                    wait(pe, s["ctx_hi"], (b + 1) * NG)
                    wait(pe, s["ctx_lo"], (b + 1) * NG)
                n = 0
                for x, a in ((0, 0), (1, 0), (0, 1)):
                    for g in range(NG):
                        last = nc.tensor.matmul(ps[:], cx[:, g, x, i * P:(i + 1) * P], wout[:, g, a, :],
                                                start=(n == 0), stop=(n == 3 * NG - 1))
                        n += 1
                last.then_inc(s["O_done"], 1)

            def scores(b, g, j):
                h = b * H + g * HG + j
                par = g % 2
                if j == 0:
                    for w in range(2):
                        wait(pe, stacked[w][par], (b * 2 + g // 2 + 1) * 64)
                for i in range(QB):
                    n = h * QB + i
                    wait(pe, s["ttr_done"], n - 1)
                    nc.tensor.matmul(psS[i % 2][:, 0:(i + 1) * P], qs[:, par, j, i * P:(i + 1) * P],
                                     ks[:, par, j, 0:(i + 1) * P], start=True, stop=True
                                     ).then_inc(s["S_done"], 1)

            def ptrans(b, g, j):
                h = b * H + g * HG + j
                wait(pe, s["norm_done"], (h + 1) * QB)
                for r, kbs in enumerate(TJOBS):
                    t = h * 3 + r
                    ps = psT[(3 * j + r) % 2]
                    wait(pe, s["T_lo"], t - 1)
                    for kb in kbs:
                        for i in range(kb, QB):
                            o = SEG[kb] - SEG[kbs[0]] + (i - kb) * P
                            c = ROWOFF[i] + kb * P
                            last = nc.tensor.transpose(ps[:, o:o + P], pr[:, j, c:c + P],
                                                       conf[:, C_ID:C_ID + P])
                    last.then_inc(s["T_done"], 1)

            def pv(b, g, par):
                u = b * NG + g
                wait(pe, s["T_lo"], (u + 1) * 12)
                if g == 0:
                    wait(pe, s["V_lo"], (b + 1) * QB)
                wait(pe, s["ctx_staged"], u)
                for kb in range(QB):
                    w = S - kb * P
                    for n, (x, a) in enumerate(((0, 0), (0, 1), (1, 0))):
                        for j in range(HG):
                            c = (g * HG + j) * HD
                            last = nc.tensor.matmul(
                                psC[j * HD:(j + 1) * HD, kb * P:S], v[:, par, a, kb, c:c + HD],
                                pt[:, g % 2, x, j, SEG[kb]:SEG[kb] + w],
                                start=(kb == 0 and n == 0), stop=(kb == QB - 1 and n == 2))
                last.then_inc(s["PV_done"], 1)

            def iteration(b, odd):
                me = (b, odd)
                nxt = b + 1
                more = within(b, -1, B - 1)
                for g in range(NG):
                    for j in range(HG):
                        if isinstance(b, int):
                            hh = b * H + g * HG + j
                            if 0 <= hh + 2 < B * H:
                                scores((hh + 2) // H, (hh + 2) // HG % NG, (hh + 2) % HG)
                        else:
                            f = g * HG + j + 2
                            scores(b if f < H else nxt, f // HG % NG, f % HG)
                        if j < 2 and g < 2:
                            qk(b, g + 2, j, (0 if g == 0 else 6) + j, me)
                        if j < 2 and g >= 2 and more:
                            if g == 3 and j == 0:
                                rank(nxt)
                            qk(nxt, g - 2, j, (12 if g == 2 else 17) + j, me)
                        if g == 0 and j >= 2 and within(b, 1, B + 1):
                            for i in (2 * j - 4, 2 * j - 3):
                                oproj(b - 1, i, 2 + i, me)
                        if g == 1 and j >= 2 and more:
                            for i in (2 * j - 4, 2 * j - 3):
                                transposes(nxt, i, 8 + i, me)
                        if g == 2 and j == 2 and more:
                            vproj(nxt, 0, 14, me)
                            router(15, me)
                        if g == 2 and j == 3 and more:
                            vproj(nxt, 1, 16, me)
                        if g == 3 and j >= 2 and more:
                            vproj(nxt, j, 17 + j, me)
                        if j == 0:
                            if g > 0 and within(b, 0, B):
                                pv(b, g - 1, odd)
                            elif g == 0 and within(b, 1, B + 1):
                                pv(b - 1, NG - 1, 1 - odd)
                        if within(b, 0, B):
                            ptrans(b, g, j)

            pe.sem_inc(s["O_done"], 1)
            pe.wait_ge(s["consts_made"], 1)
            pe.wait_ge(s["w_split_hi"], 3)
            pe.wait_ge(s["w_split_lo"], 3)
            batches(pe, iteration)

        @block.scalar
        def _(act):
            act.wait_ge(s["scales"], 1)
            for dst, src, c in ((wqkv, wq_f, X_SWQ), (wout, wo_f, X_SWO), (wr, wr_f[:, :], X_SWR)):
                n = dst.shape[3]
                nc.scalar.activation(dst[:, :, 0, :], src.rearrange("p (k n) -> p k n", n=n), ACT.Copy,
                                     scale=sc[:, c:c + 1]).then_inc(s["w_split_hi"], 1)

            def stage_qk(b, g, w):
                if not within(b, 0, B):
                    return
                u = b * NG + g
                wait(act, s["qk_done"], u * 2 + 1 + w)
                wait(act, s["qk_lo"], u * 2 - 1 + w)
                wait(act, s["qk_hi"], u * 2 - 1 + w)
                scale = cq[:, g:g + 1] if w == 0 else sc[:, X_CK:X_CK + 1]
                nc.scalar.activation(stage[:, w, :], psA[bankof(g, w)][:], ACT.Identity,
                                     bias=bqs[:, w * NG + g:w * NG + g + 1], scale=scale
                                     ).then_inc(s["qk_staged"], 1)

            def xhi(b, par, i):
                wait(act, s["xT_done"], b * QB + i + 1)
                nc.scalar.activation(xT[:, par, 0, :, i * P:(i + 1) * P],
                                     psA[(8 + i) % ABANKS][:].rearrange("p (k n) -> p k n", k=KC),
                                     ACT.Copy, scale=1024.0).then_inc(s["xT_hi"], 1)

            def vhi(b, par, i):
                wait(act, s["V_done"], b * QB + i + 1)
                wait(act, s["PV_done"], (b - 1) * NG)
                nc.scalar.activation(v[:, par, 0, i, :], psA[(14, 16, 19, 20)[i] % ABANKS][:], ACT.Copy,
                                     scale=2.0 ** -19).then_inc(s["V_hi"], 1)

            def iteration(b, odd):
                nxt, par = b + 1, 1 - odd
                more = within(b, -1, B - 1)
                for g in range(NG):
                    for j in range(HG):
                        f = g * HG + j + 2
                        hb, h16 = (b, f) if f < H else (nxt, f - H)
                        if within(hb, 0, B):
                            for i in range(QB):
                                c, n = (h16 % HG) * QB + i, (hb * H + h16) * QB + i
                                wait(act, s["ttr_done"], n + 1)
                                wait(act, s["rden_done"], hb * H + h16 - HG + 1)
                                p_ = pr[:, h16 % HG, ROWOFF[i]:ROWOFF[i] + (i + 1) * P]
                                nc.scalar.activation(p_, p_, ACT.Exp, bias=mn[:, c:c + 1], scale=-1.0,
                                                     accum_out=den[:, c:c + 1]).then_inc(s["exp_done"], 1)
                        if j < 2 and g < 2:
                            stage_qk(b, g + 2, j)
                        if j < 2 and g >= 2 and more:
                            stage_qk(nxt, g - 2, j)
                        if g == 1 and j >= 2 and more:
                            for i in (2 * j - 4, 2 * j - 3):
                                if i == 0:
                                    wait(act, s["V_done"], b * QB)
                                    wait(act, s["qk_done"], b * 8)
                                    wait(act, s["R_done"], b)
                                xhi(nxt, par, i)
                        if g == 2 and j == 2 and more:
                            vhi(nxt, par, 0)
                        if g == 2 and j == 3 and more:
                            vhi(nxt, par, 1)
                            wait(act, s["nd_ready"], b + 2)
                            nc.scalar.activation(ex[:], nd[:], ACT.Exp).then_inc(s["rexp_done"], 1)
                        if g == 3 and j >= 2 and more:
                            vhi(nxt, par, j)
                        pb, pg = (b, g - 1) if g > 0 else (b - 1, NG - 1)
                        if j == 0 and within(pb, 0, B):
                            u = pb * NG + pg
                            wait(act, s["PV_done"], u + 1)
                            wait(act, s["ctx_hi"], u)
                            wait(act, s["ctx_lo"], u)
                            nc.scalar.activation(cf[:], psC[:], ACT.Identity,
                                                 bias=bqs[:, 2 * NG + pg:2 * NG + pg + 1],
                                                 scale=sc[:, X_CC:X_CC + 1]).then_inc(s["ctx_staged"], 1)
                        if within(b, 0, B):
                            hd = b * H + g * HG + j
                            wait(act, s["PV_done"], b * NG + g - 1)
                            for r, kbs in enumerate(TJOBS):
                                w = sum(S - kb * P for kb in kbs)
                                o = SEG[kbs[0]]
                                wait(act, s["T_done"], hd * 3 + r + 1)
                                nc.scalar.activation(pt[:, g % 2, 0, j, o:o + w],
                                                     psT[(3 * j + r) % 2][:, 0:w], ACT.Copy
                                                     ).then_inc(s["T_hi"], 1)

            batches(act, iteration)

        @block.vector
        def _(dve):
            n_setup = [0]

            def setup(ins):
                n_setup[0] += 1
                ins.then_inc(s["setup"], 1)
                dve.wait_ge(s["setup"], n_setup[0])

            dve.wait_ge(s["const_in"], 16)
            nc.vector.memset(half[:], -0.5)
            nc.vector.memset(esum[:], 0.0)
            nc.vector.memset(fam[:], 0.0)
            nc.vector.memset(ones16[:], 1.0)
            nc.vector.memset(e16[:], 0.0)
            nc.vector.memset(epre[:], 0.0)
            nc.vector.memset(am[:], 0.0)
            nc.vector.memset(meta[:], 0.0)
            nc.vector.tensor_copy(tid[:], conf[:, C_TOK:C_TOK + QB])
            setup(nc.vector.tensor_copy(lt16[:], conf[:, C_LT:C_LT + P]))
            n_setup[0] += 1
            nc.vector.memset(t0[:], 0.0).then_inc(s["setup"], 1)
            dve.wait_ge(s["setup"], n_setup[0])

            dve.wait_ge(s["w_in"], 32)
            dve.wait_ge(s["wr_in"], 48)
            for c, src in ((0, wq_f), (1, bqk[:, :]), (2, wo_f), (3, wr_f[:, :])):
                setup(nc.vector.tensor_reduce(am[:, c:c + 1], src, AX.X, ALU.max, apply_absolute_value=True))
            nc.vector.tensor_scalar(am[:, 0:4], am[:, 0:4], 1.0, None, ALU.mult).then_inc(s["absmax"], 1)
            dve.wait_ge(s["allmax"], 1)
            x = lambda c, n=1: sc[:, c:c + n]

            def pow2(dst, src):
                setup(nc.vector.tensor_scalar(dst.bitcast(I32), src.bitcast(I32), 0x7F800000, None,
                                              ALU.bitwise_and))

            ts = nc.vector.tensor_scalar
            setup(ts(amr[:, 0:4], amr[:, 0:4], 1e-9, None, ALU.max))
            setup(ts(x(X_T0), amr[:, 0:1], float(D), amr[:, 1:2], ALU.mult, ALU.add))
            pow2(x(X_PA), amr[:, 0:1])
            pow2(x(X_PM), x(X_T0))
            pow2(x(X_PAO), amr[:, 2:3])
            pow2(x(X_PAR), amr[:, 3:4])
            for dst, src in ((X_SWQ, X_PA), (X_SWO, X_PAO), (X_SWR, X_PAR), (X_RPM, X_PM)):
                setup(nc.vector.reciprocal(x(dst), x(src)))
            setup(ts(x(X_SWQ, 3), x(X_SWQ, 3), 2.0 ** 14, None, ALU.mult))
            setup(ts(x(X_T1), x(X_RPM), x(X_PA), None, ALU.mult))
            setup(ts(x(X_CK), x(X_T1), 2.0 ** -10, None, ALU.mult))
            setup(ts(x(X_CC), x(X_T1), 2.0 ** -6, None, ALU.mult))
            setup(nc.vector.tensor_tensor(x(X_CS), x(X_PM), x(X_PAO), ALU.mult))
            setup(ts(x(X_CS), x(X_CS), 2.0 ** -28, None, ALU.mult))
            setup(ts(x(X_CR), x(X_PAR), 2.0 ** -24, None, ALU.mult))
            setup(ts(cq[:], conf[:, C_F:C_F + NG], x(X_T1), None, ALU.mult))
            setup(ts(cq[:], cq[:], 2.0 ** -16, None, ALU.mult))
            setup(ts(bqs[:], bqk[:], x(X_RPM), None, ALU.mult))
            setup(ts(bqs[:], bqs[:], 2.0 ** 14, None, ALU.mult))
            setup(nc.vector.tensor_tensor(bqs[:, 0:NG], bqs[:, 0:NG], conf[:, C_F:C_F + NG], ALU.mult))
            setup(ts(bqs[:, 0:NG], bqs[:, 0:NG], 2.0 ** -6, None, ALU.mult))
            setup(nc.vector.tensor_tensor(x(X_T0), x(X_PM), x(X_PM), ALU.mult))
            setup(ts(x(X_T0), x(X_T0), 2.0 ** -22, None, ALU.mult))
            setup(ts(nsl[:], conf[:, C_NSL:C_NSL + H], x(X_T0), None, ALU.mult))
            setup(nc.vector.reciprocal(x(X_T0), x(X_T0)))
            setup(ts(base[:], conf[:, C_BASE:C_BASE + S], x(X_T0), None, ALU.mult))
            nc.vector.memset(t1[:], 0.0).then_inc(s["scales"], 1)
            for n, (dst, src, c) in enumerate(((wqkv, wq_f, X_SWQ), (wout, wo_f, X_SWO), (wr, wr_f[:, :], X_SWR))):
                dve.wait_ge(s["w_split_hi"], n + 1)
                w3 = src.rearrange("p (k n) -> p k n", n=dst.shape[3])
                nc.vector.scalar_tensor_tensor(out=dst[:, :, 1, :], in0=w3, scalar=x(c), in1=dst[:, :, 0, :],
                                               op0=ALU.mult, op1=ALU.subtract).then_inc(s["w_split_lo"], 1)
            nc.vector.memset(t1[:], 0.0).then_inc(s["consts_made"], 1)

            LINKS = 18

            def iteration(b, odd):
                nxt, par = b + 1, 1 - odd
                more = within(b, -1, B - 1)
                k = [0]

                def link(ins):
                    k[0] += 1
                    ins.then_inc(s["dve_link"], 1)
                    wait(dve, s["dve_link"], (b + 1) * LINKS + k[0], s["apart_dve"])

                def ln_stats(i):
                    wait(dve, x_in[i], (nxt + 1) * 16)
                    link(nc.vector.bn_stats(stat[:, i, :], xin[:, i, :]))
                    nc.vector.bn_aggr(mv[:, i, :], stat[:, i, :]).then_inc(s["ln_stats"], 1)

                def ln_apply(i):
                    if i == 0:
                        wait(dve, s["rstd_ready"], nxt + 1)
                    wait(dve, s["xT_done"], b * QB + i + 1)
                    nc.vector.tensor_scalar(xn[:, i, :], xin[:, i, :], mv[:, i, 0:1], rstd[:, par, i:i + 1],
                                            ALU.subtract, ALU.mult).then_inc(s["xn_ready"], 1)

                def xlo(i):
                    wait(dve, s["xT_hi"], nxt * QB + i + 1)
                    nc.vector.scalar_tensor_tensor(
                        out=xT[:, par, 1, :, i * P:(i + 1) * P],
                        in0=psA[(8 + i) % ABANKS][:].rearrange("p (k n) -> p k n", k=KC), scalar=1024.0,
                        in1=xT[:, par, 0, :, i * P:(i + 1) * P], op0=ALU.mult, op1=ALU.subtract
                    ).then_inc(s["xT_lo"], 1)

                def vlo(i):
                    wait(dve, s["V_hi"], nxt * QB + i + 1)
                    nc.vector.scalar_tensor_tensor(
                        out=v[:, par, 1, i, :], in0=psA[(14, 16, 19, 20)[i] % ABANKS][:], scalar=2.0 ** -19,
                        in1=v[:, par, 0, i, :], op0=ALU.mult, op1=ALU.subtract).then_inc(s["V_lo"], 1)

                def qk_hi(bq, g, w):
                    if not within(bq, 0, B):
                        return
                    u = bq * NG + g
                    wait(dve, s["qk_staged"], u * 2 + 1 + w)
                    wait(dve, stored[w], u * 16)
                    nc.vector.tensor_copy(pre[:, w, 0, :], stage[:, w, :]).then_inc(s["qk_hi"], 1)

                def choose():
                    psr = psA[15 % ABANKS]
                    wait(dve, s["R_done"], nxt + 1)
                    wait(dve, s["R2_done"], nxt)
                    link(ts(lg[:].rearrange("p i e -> p (i e)"), psr[:, 0:QB * E], x(X_CR), None, ALU.mult))
                    link(nc.vector.tensor_tensor(dl[:], lg[:, :, 1], lg[:, :, 0], ALU.subtract))
                    nc.vector.scalar_tensor_tensor(out=nd[:], in0=dl[:], scalar=-1.0, in1=dl[:],
                                                   op0=ALU.mult, op1=ALU.min).then_inc(s["nd_ready"], 1)
                    link(ts(ef[:, 0:QB], dl[:], 0.0, None, ALU.is_gt))
                    nc.vector.tensor_copy(e16[:, 0:QB], ef[:, 0:QB])
                    link(nc.vector.tensor_copy(epre[:, 1:2], ef[:, 0:1]))
                    for i in range(1, QB):
                        link(nc.vector.tensor_tensor(epre[:, i + 1:i + 2], epre[:, i:i + 1], ef[:, i:i + 1],
                                                     ALU.add))
                    nc.vector.memset(t0[:, 0:1], 0.0).then_inc(s["e_ready"], 1)

                def place():
                    psr = psA[15 % ABANKS]
                    wait(dve, s["R2_done"], nxt + 1)
                    wait(dve, s["rexp_done"], nxt + 1)
                    wait(dve, s["meta_out"], nxt * QB * 16)
                    nc.vector.tensor_scalar(rk[:], psr[:, 16:16 + QB + 1], esum[:, 0:1], None, ALU.add
                                            ).then_inc(s["rank_read"], 1)
                    dve.wait_ge(s["rank_read"], nxt + 1)
                    nc.vector.tensor_copy(esum[:, 0:1], rk[:, QB:QB + 1])
                    link(nc.vector.tensor_tensor(t0[:], tid[:], rk[:, 0:QB], ALU.subtract))
                    link(ts(t1[:], tid[:], -1.0, float(TOK - 1), ALU.mult, ALU.add))
                    link(nc.vector.tensor_tensor(t1[:], t1[:], ef[:, 0:QB], ALU.mult))
                    link(nc.vector.tensor_tensor(t0[:], t0[:], t1[:], ALU.add))
                    nc.vector.tensor_copy(pos[:], t0[:])
                    nc.vector.tensor_copy(meta[:, :, 0], tid[:])
                    link(ts(t1[:], ex[:], 1.0, None, ALU.add))
                    nc.vector.tensor_copy(meta[:, :, 2], ef[:, 0:QB])
                    nc.vector.tensor_copy(meta[:, :, 3], mv[:, :, 0])
                    nc.vector.tensor_copy(meta[:, :, 4], rstd[:, par, :])
                    link(nc.vector.reciprocal(meta[:, :, 1], t1[:]))
                    link(ts(tid[:], tid[:], float(S), None, ALU.add))
                    nc.vector.memset(rk[:, 0:1], 0.0).then_inc(s["meta_ready"], 1)

                for g in range(NG):
                    for j in range(HG):
                        hd = b * H + g * HG + j
                        f = g * HG + j + 1
                        rb, r16 = (b, f) if f < H else (nxt, f - H)
                        if within(rb, 0, B):
                            wait(dve, s["exp_done"], (rb * H + r16 + 1) * QB)
                            wait(dve, s["norm_done"], (rb * H + r16 - HG + 1) * QB)
                            c = (r16 % HG) * QB
                            nc.vector.reciprocal(rden[:, c:c + QB], den[:, c:c + QB]).then_inc(s["rden_done"], 1)
                        f = g * HG + j + 2
                        hb, h16 = (b, f) if f < H else (nxt, f - H)
                        if within(hb, 0, B):
                            hh = hb * H + h16
                            wait(dve, s["T_done"], (hh - HG + 1) * 3)
                            for i in range(QB):
                                w = (i + 1) * P
                                c = (h16 % HG) * QB + i
                                wait(dve, s["S_done"], hh * QB + i + 1, s["apart_dve"])
                                nc.vector.tensor_tensor_reduce(
                                    out=pr[:, h16 % HG, ROWOFF[i]:ROWOFF[i] + w], in0=psS[i % 2][:, 0:w],
                                    in1=base[:, S - w:S], scale=nsl[:, h16:h16 + 1], scalar=3e38,
                                    op0=ALU.add, op1=ALU.min, accum_out=mn[:, c:c + 1]
                                ).then_inc(s["ttr_done"], 1)
                        if more:
                            if g == 0 and j >= 2:
                                ln_stats(2 * j - 4)
                                ln_stats(2 * j - 3)
                            if g == 1 and j < 2:
                                ln_apply(2 * j)
                                ln_apply(2 * j + 1)
                            if g == 1 and j >= 2:
                                xlo(2 * j - 4)
                                xlo(2 * j - 3)
                            if g == 2 and j == 2:
                                vlo(0)
                                choose()
                            if g == 2 and j == 3:
                                vlo(1)
                            if g == 3 and j == 0:
                                place()
                            if g == 3 and j >= 2:
                                vlo(j)
                        if g == 0 and j >= 2 and within(b, 1, B + 1):
                            for i in (2 * j - 4, 2 * j - 3):
                                wait(dve, s["O_done"], (b - 1) * QB + i + 2)
                                wait(dve, s_out[i], b * 16)
                                nc.vector.scalar_tensor_tensor(
                                    out=so[:, i, :], in0=psA[(2 + i) % ABANKS][:], scalar=x(X_CS),
                                    in1=bout[:], op0=ALU.mult, op1=ALU.add).then_inc(s["O_evac"], 1)
                        if within(b, 0, B) and (g, j) in ((1, 0), (3, 1)):
                            c = g // 2
                            wait(dve, s["wmax_in"], (b * 2 + c + 1) * 16)
                            nc.vector.tensor_reduce(fam[:, 2:3], wst[:], AX.X, ALU.max,
                                                    apply_absolute_value=True).then_inc(s["wmax_done"], 1)
                            dve.wait_ge(s["wmax_done"], b * 2 + c + 1)
                            nc.vector.tensor_tensor(fam[:, c:c + 1], fam[:, c:c + 1], fam[:, 2:3], ALU.max
                                                    ).then_inc(s["wm_link"], 1)
                            dve.wait_ge(s["wm_link"], b * 2 + c + 1)
                        if within(b, 0, B):
                            for r, kbs in enumerate(TJOBS):
                                w = sum(S - kb * P for kb in kbs)
                                o = SEG[kbs[0]]
                                wait(dve, s["T_hi"], hd * 3 + r + 1)
                                nc.vector.tensor_tensor(pt[:, g % 2, 1, j, o:o + w],
                                                        psT[(3 * j + r) % 2][:, 0:w],
                                                        pt[:, g % 2, 0, j, o:o + w], ALU.subtract
                                                        ).then_inc(s["T_lo"], 1)
                        pb, pg = (b, g - 1) if g > 0 else (b - 1, NG - 1)
                        if j == 0 and within(pb, 0, B):
                            wait(dve, s["ctx_staged"], pb * NG + pg + 1)
                            wait(dve, s["O_done"], pb * QB + 1)
                            nc.vector.tensor_copy(cx[:, pg, 0, :], cf[:]).then_inc(s["ctx_hi"], 1)
                        if j < 2 and g < 2:
                            qk_hi(b, g + 2, j)
                        if j < 2 and g >= 2 and more:
                            qk_hi(nxt, g - 2, j)
                assert not more or k[0] == LINKS, k[0]

            batches(dve, iteration)

        @block.gpsimd
        def _(pool):
            pool.wait_ge(s["absmax"], 1)
            nc.gpsimd.partition_all_reduce(amr[:, 0:4], am[:, 0:4], P, RMAX).then_inc(s["allmax"], 1)

            def qk_lo(b, g, w):
                if not within(b, 0, B):
                    return
                u = b * NG + g
                wait(pool, s["qk_hi"], u * 2 + 1 + w, s["apart_pool"])
                nc.gpsimd.tensor_tensor(pre[:, w, 1, :], stage[:, w, :], pre[:, w, 0, :], ALU.subtract
                                        ).then_inc(s["qk_lo"], 1)

            def iteration(b, odd):
                nxt, par = b + 1, 1 - odd
                more = within(b, -1, B - 1)
                for g in range(NG):
                    for j in range(HG):
                        f = g * HG + j + 1
                        rb, r16 = (b, f) if f < H else (nxt, f - H)
                        if within(rb, 0, B):
                            wait(pool, s["rden_done"], rb * H + r16 + 1, s["apart_pool"])
                            for i in range(QB):
                                c = (r16 % HG) * QB + i
                                p_ = pr[:, r16 % HG, ROWOFF[i]:ROWOFF[i] + (i + 1) * P]
                                nc.gpsimd.tensor_scalar(p_, p_, rden[:, c:c + 1], 32768.0, ALU.mult, ALU.mult
                                                        ).then_inc(s["norm_done"], 1)
                        if more and g == 0 and j == 3:
                            wait(pool, s["ln_stats"], (nxt + 1) * QB, s["apart_pool"])
                            wait(pool, s["meta_ready"], nxt - 1, s["apart_pool"])
                            nc.gpsimd.tensor_scalar(veps[:], mv[:, :, 1], 1e-5, 1.0, ALU.add, ALU.mult
                                                    ).then_inc(s["pool_link"], 1)
                            wait(pool, s["pool_link"], nxt + 1, s["apart_pool"])
                            nc.gpsimd.tensor_tensor(rstd[:, par, :], veps[:], half[:], ALU.pow
                                                    ).then_inc(s["rstd_ready"], 1)
                        pb, pg = (b, g - 1) if g > 0 else (b - 1, NG - 1)
                        if j == 0 and within(pb, 0, B):
                            wait(pool, s["ctx_hi"], pb * NG + pg + 1, s["apart_pool"])
                            nc.gpsimd.tensor_tensor(cx[:, pg, 1, :], cf[:], cx[:, pg, 0, :], ALU.subtract
                                                    ).then_inc(s["ctx_lo"], 1)
                        if j < 2 and g < 2:
                            qk_lo(b, g + 2, j)
                        if j < 2 and g >= 2 and more:
                            qk_lo(nxt, g - 2, j)
                        if more and g == 3 and j == 2:
                            wait(pool, s["meta_ready"], nxt + 1, s["apart_pool"])
                            for i in range(QB):
                                nc.gpsimd.indirect_dma_start(
                                    out=io["meta"], out_offset=bass.IndirectOffsetOnAxis(ap=pos[:, i:i + 1], axis=0),
                                    in_=meta[:, i, :], in_offset=None).then_inc(s["meta_out"], 16)

            batches(pool, iteration)
            pool.wait_ge(s["meta_out"], 16 * QB * B)
            pool.wait_ge(s["wm_link"], 2 * B)
            nc.gpsimd.partition_all_reduce(sc[:, X_PA1:X_PA1 + 2], fam[:, 0:2], P, RMAX
                                           ).then_inc(s["allmax"], 1)
            pool.wait_ge(s["allmax"], 2)


def ffn_block(nc, io, sc, conf, esum):
    with ExitStack() as ctx:
        sb = lambda n, s, d: ctx.enter_context(nc.sbuf_tensor(n, s, d))
        sem = lambda n: ctx.enter_context(nc.semaphore(n))
        NP = 2 * HC
        wf = sb("wf", [P, E, NP, 2, 2048], F16)
        wstage = sb("wstage", [P, 2, 2048], F32)
        mall = sb("mall", [P, TOK // P, MROW], F32)
        eslot = sb("eslot", [P, SLOTS], F32)
        eint = sb("eint", [P, SLOTS], I32)
        tint = sb("tint", [P, SLOTS], I32)
        n0 = sb("n0", [P, 1], F32)
        rec = sb("rec", [P, 4, MROW], F32)
        gidx = sb("gidx", [P, 4], I32)
        oidx = sb("oidx", [P, 2], I32)
        miss = sb("miss", [P, 1], F32)
        xg = sb("xg", [P, 4, D], F32)
        sg = sb("sg", [P, 2, D], F32)
        xn = sb("xn2", [P, D], F32)
        xT = sb("xT2", [P, 2, 2, D], F16)
        rl = sb("rl", [P, 2, 512], F32)
        a = sb("a", [P, 2, HC, 512], F32)
        aT = sb("aT", [P, 2, 2, 512], F16)
        z = sb("z", [P, D], F32)
        gt = sb("gt", [P, D], F32)
        ob = sb("ob", [P, D], F32)
        psF = [ctx.enter_context(nc.psum_tensor(f"psF{i}", [P, 512], F32)) for i in range(2)]
        psT = [ctx.enter_context(nc.psum_tensor(f"psU{i}", [P, 512], F32)) for i in range(2)]
        psX = ctx.enter_context(nc.psum_tensor("psX", [P, 512], F32))
        psY = [ctx.enter_context(nc.psum_tensor(f"psY{i}", [P, 512], F32)) for i in range(2)]
        names = ("m_in made ws_hi ws_lo e_table idx_ready ln_done X_done X_hi X_lo F_done f_relu f_sum "
                 "a_ready U_done U_hi U_lo Y_done z_ready g_exp g_ready o_ready ob_free apart_pool f_link out_done").split()
        s = {n: sem("f_" + n) for n in names}
        w_in = [sem(f"wf_in{i}") for i in range(2)]
        x_got = [sem(f"x_got{i}") for i in range(4)]
        s_got = [sem(f"s_got{i}") for i in range(2)]
        block = ctx.enter_context(nc.Block())
        LOOPS = (SLOTS - 4) // 4

        def arrived(n, r, ring):
            return (n - (r % ring) + ring) * (16 // ring)

        def slots(eng, step):
            for n in range(-3, 1):
                step(n, n % 4)
            with eng.Fori(0, LOOPS) as it:
                for q in range(4):
                    step(it * 4 + (q + 1), (q + 1) % 4)
            for n in range(4 * LOOPS + 1, SLOTS + 1):
                step(n, n % 4)

        @block.sync
        def _(sp):
            for n in range(E * NP):
                if n >= 2:
                    sp.wait_ge(s["ws_lo"], n - 1)
                sp.dma_start(wstage[:, n % 2, :], io["wf"][n]).then_inc(w_in[n % 2], 16)
                if n == 0:
                    sp.dma_start(mall[:], io["meta"].rearrange("(t p) c -> p t c", p=P)).then_inc(s["m_in"], 16)

        @block.tensor
        def _(pe):
            def expert(eng_s):
                return pe.value_load(eint[0:1, bass.ds(eng_s, 1)], min_val=0, max_val=1)

            def w(e, piece, hl, c):
                return wf[:, bass.ds(e, 1), piece, hl, c * 512:(c + 1) * 512].rearrange("p o n -> p (o n)")

            def xtrans(n, r):
                wait(pe, s["ln_done"], n + 1)
                wait(pe, s["X_lo"], n)
                for kc in range(KC):
                    last = nc.tensor.transpose(psX[:, kc * P:(kc + 1) * P], xn[:, kc * P:(kc + 1) * P],
                                               conf[:, C_ID:C_ID + P])
                last.then_inc(s["X_done"], 1)

            def up(n, r, hc, e):
                t = n * HC + hc
                if hc == 0:
                    wait(pe, s["X_lo"], n + 1)
                if isinstance(n, int):
                    wait(pe, s["ws_lo"], 2 * hc + 1 + (NP if n > 0 else 0))
                ps = psF[hc % 2]
                wait(pe, s["f_sum"], t - 1)
                k = 0
                for x, hl in ((0, 0), (1, 0), (0, 1)):
                    for kc in range(KC):
                        last = nc.tensor.matmul(ps[:], xT[:, r % 2, x, kc * P:(kc + 1) * P],
                                                w(e, 2 * hc, hl, kc), start=(k == 0), stop=(k == 3 * KC - 1))
                        k += 1
                last.then_inc(s["F_done"], 1)

            def turn(n, r, hc):
                t = n * HC + hc
                wait(pe, s["a_ready"], t + 1)
                wait(pe, s["U_lo"], t - 1)
                for q in range(4):
                    last = nc.tensor.transpose(psT[hc % 2][:, q * P:(q + 1) * P],
                                               a[:, r % 2, hc, q * P:(q + 1) * P], conf[:, C_ID:C_ID + P])
                last.then_inc(s["U_done"], 1)

            def down(n, r, hc, e):
                t = n * HC + hc
                if hc == 0:
                    wait(pe, s["z_ready"], n)
                if isinstance(n, int):
                    wait(pe, s["ws_lo"], 2 * hc + 2 + (NP if n > 0 else 0))
                wait(pe, s["U_lo"], t + 1)
                k = 0
                for x, hl in ((0, 0), (1, 0), (0, 1)):
                    for q in range(4):
                        last = nc.tensor.matmul(psY[r % 2][:], aT[:, hc % 2, x, q * P:(q + 1) * P],
                                                w(e, 2 * hc + 1, hl, q), start=(hc == 0 and k == 0),
                                                stop=(hc == HC - 1 and k == 11))
                        k += 1
                last.then_inc(s["Y_done"], 1)

            def step(n, r):
                here, ahead = within(n, 0, SLOTS), within(n + 1, 0, SLOTS)
                e0 = expert(n) if here else None
                e1 = expert(n + 1) if ahead else None
                if ahead and not isinstance(n, int):
                    pe.wait_ge(s["ws_lo"], E * NP)
                for hc in range(HC):
                    if here:
                        turn(n, r, hc)
                    if here and hc > 0:
                        down(n, r, hc - 1, e0)
                    if ahead:
                        up(n + 1, r + 1, hc, e1)
                if within(n + 2, 0, SLOTS):
                    xtrans(n + 2, r + 2)
                if here:
                    down(n, r, HC - 1, e0)

            pe.wait_ge(s["e_table"], 1)
            slots(pe, step)

        @block.scalar
        def _(act):
            act.wait_ge(s["made"], 1)

            def split(e):
                for q in range(NP):
                    n = e * NP + q
                    act.wait_ge(w_in[n % 2], (n // 2 + 1) * 16)
                    c = X_S1 + q % 2
                    nc.scalar.activation(wf[:, e, q, 0, :], wstage[:, n % 2, :], ACT.Copy, scale=sc[:, c:c + 1]
                                         ).then_inc(s["ws_hi"], 1)

            def relu(n, r, hc):
                t = n * HC + hc
                wait(act, s["F_done"], t + 1)
                wait(act, s["f_sum"], t - 1)
                nc.scalar.activation(rl[:, hc % 2, :], psF[hc % 2][:], ACT.Relu, scale=2.0 ** -28
                                     ).then_inc(s["f_relu"], 1)

            def uhi(n, r, hc):
                t = n * HC + hc
                wait(act, s["U_done"], t + 1)
                wait(act, s["Y_done"], t - 1)
                nc.scalar.activation(aT[:, hc % 2, 0, :], psT[hc % 2][:], ACT.Copy).then_inc(s["U_hi"], 1)

            def step(n, r):
                here, ahead = within(n, 0, SLOTS), within(n + 1, 0, SLOTS)
                if isinstance(n, int) and n == -1:
                    split(0)
                for hc in range(HC):
                    if here:
                        uhi(n, r, hc)
                    if ahead:
                        relu(n + 1, r + 1, hc)
                    if hc == 1 and within(n - 1, 0, SLOTS):
                        wait(act, s["z_ready"], n + 1)
                        nc.scalar.activation(gt[:], gt[:], ACT.Exp, scale=-1.0).then_inc(s["g_exp"], 1)
                if isinstance(n, int) and n == -1:
                    split(1)
                if within(n + 2, 0, SLOTS):
                    wait(act, s["X_done"], n + 3)
                    wait(act, s["F_done"], (n + 1) * HC)
                    nc.scalar.activation(xT[:, r % 2, 0, :], psX[:], ACT.Copy, scale=1024.0
                                         ).then_inc(s["X_hi"], 1)

            slots(act, step)

        @block.vector
        def _(dve):
            n_made = [0]

            def made(ins):
                n_made[0] += 1
                ins.then_inc(s["f_link"], 1)
                dve.wait_ge(s["f_link"], n_made[0])

            ts = nc.vector.tensor_scalar
            x = lambda c, n=1: sc[:, c:c + n]
            made(ts(x(X_PA1, 2), x(X_PA1, 2), 1e-9, None, ALU.max))
            made(ts(x(X_PA1, 2).bitcast(I32), x(X_PA1, 2).bitcast(I32), 0x7F800000, None, ALU.bitwise_and))
            made(nc.vector.reciprocal(x(X_S1, 2), x(X_PA1, 2)))
            made(ts(x(X_S1, 2), x(X_S1, 2), 2.0 ** 14, None, ALU.mult))
            made(nc.vector.tensor_tensor(x(X_CY), x(X_PA1), x(X_PA1), ALU.mult))
            made(nc.vector.tensor_tensor(x(X_CY), x(X_CY), x(X_PA2), ALU.mult))
            made(ts(x(X_CY), x(X_CY), 2.0 ** -8, None, ALU.mult))
            made(ts(n0[:], esum[:, 0:1], -1.0, float(TOK), ALU.mult, ALU.add))
            made(ts(n0[:], n0[:], float(TOK - 1), None, ALU.min))
            made(ts(eslot[:], conf[:, C_SLOT:C_SLOT + SLOTS], n0[:, 0:1], None, ALU.is_gt))
            made(nc.vector.tensor_copy(eint[:], eslot[:]))
            made(nc.vector.scalar_tensor_tensor(out=tint[:], in0=conf[:, C_SLOT:C_SLOT + SLOTS], scalar=1.0 / P,
                                                in1=eslot[:], op0=ALU.mult, op1=ALU.subtract))
            nc.vector.memset(miss[:], 0.0).then_inc(s["made"], 1)
            nc.vector.memset(z[:], 0.0).then_inc(s["e_table"], 1)
            nc.vector.memset(ob[:, 0:1], 0.0).then_inc(s["z_ready"], 1)
            dve.wait_ge(s["m_in"], 16)
            MADE = n_made[0]
            LK = 7

            def split(e):
                for q in range(NP):
                    n = e * NP + q
                    dve.wait_ge(s["ws_hi"], n + 1)
                    c = X_S1 + q % 2
                    nc.vector.scalar_tensor_tensor(out=wf[:, e, q, 1, :], in0=wstage[:, n % 2, :],
                                                   scalar=sc[:, c:c + 1], in1=wf[:, e, q, 0, :],
                                                   op0=ALU.mult, op1=ALU.subtract).then_inc(s["ws_lo"], 1)

            def fetch(n, r):
                tile = dve.value_load(tint[0:1, bass.ds(n, 1)], min_val=0, max_val=TOK // P - 1)
                src = mall[:, bass.ds(tile, 1), :].rearrange("p o c -> p (o c)")
                nc.vector.tensor_copy(rec[:, r % 4, :], src)
                nc.vector.tensor_copy(gidx[:, r % 4:r % 4 + 1], src[:, 0:1]).then_inc(s["idx_ready"], 1)

            def total(n, r, hc):
                t = n * HC + hc
                wait(dve, s["f_relu"], t + 1)
                wait(dve, s["U_done"], t - 2 * HC + 1)
                nc.vector.scalar_tensor_tensor(out=a[:, r % 2, hc, :], in0=psF[hc % 2][:], scalar=2.0 ** -28,
                                               in1=rl[:, hc % 2, :], op0=ALU.mult, op1=ALU.add
                                               ).then_inc(s["f_sum"], 1)

            def ulo(n, r, hc):
                t = n * HC + hc
                wait(dve, s["U_hi"], t + 1)
                nc.vector.tensor_tensor(aT[:, hc % 2, 1, :], psT[hc % 2][:], aT[:, hc % 2, 0, :], ALU.subtract
                                        ).then_inc(s["U_lo"], 1)

            def step(n, r):
                here, ahead = within(n, 0, SLOTS), within(n + 1, 0, SLOTS)
                done = within(n - 1, 0, SLOTS)
                k = [0]

                def link(ins):
                    k[0] += 1
                    ins.then_inc(s["f_link"], 1)
                    dve.wait_ge(s["f_link"], (n - 1) * LK + k[0] + MADE)

                if isinstance(n, int) and n == -1:
                    split(0)
                if done:
                    m = n - 1
                    rm = (r - 1) % 4
                    wait(dve, s["Y_done"], n * HC)
                    link(ts(z[:], psY[rm % 2][:], rec[:, rm, 1:2], x(X_CY), ALU.mult, ALU.mult))
                    nc.vector.tensor_scalar(gt[:], z[:], -80.0, None, ALU.max).then_inc(s["z_ready"], 1)
                for hc in range(HC):
                    if here:
                        ulo(n, r, hc)
                    if ahead:
                        total(n + 1, r + 1, hc)
                    if done and hc == 1:
                        wait(dve, s["g_exp"], n)
                        link(ts(gt[:], gt[:], 1.0, None, ALU.add))
                        link(nc.vector.reciprocal(gt[:], gt[:]))
                    if done and hc == 2:
                        wait(dve, s_got[rm % 2], arrived(n - 1, rm, 2))
                        wait(dve, s["ob_free"], n)
                        link(nc.vector.tensor_tensor(z[:], z[:], gt[:], ALU.mult))
                        link(nc.vector.tensor_tensor(z[:], z[:], sg[:, rm % 2, :], ALU.mult))
                        link(ts(miss[:], rec[:, rm, 2:3], esl(n - 1), float(OOB), ALU.not_equal, ALU.mult))
                        link(nc.vector.tensor_tensor(oidx[:, rm % 2:rm % 2 + 1], miss[:], rec[:, rm, 0:1],
                                                     ALU.add))
                        nc.vector.tensor_tensor(ob[:], z[:], xg[:, rm, :], ALU.add).then_inc(s["o_ready"], 1)
                        dve.wait_ge(s["o_ready"], n)
                if isinstance(n, int) and n == -1:
                    split(1)
                if within(n + 3, 0, SLOTS):
                    fetch(n + 3, r + 3)
                if within(n + 2, 0, SLOTS):
                    r2 = (r + 2) % 4
                    wait(dve, x_got[r2], arrived(n + 2, r2, 4))
                    wait(dve, s["X_done"], n + 2)
                    dve.wait_ge(s["idx_ready"], n + 3)
                    nc.vector.tensor_scalar(xn[:], xg[:, r2, :], rec[:, r2, 3:4], rec[:, r2, 4:5],
                                            ALU.subtract, ALU.mult).then_inc(s["ln_done"], 1)
                    wait(dve, s["X_hi"], n + 3)
                    nc.vector.scalar_tensor_tensor(out=xT[:, r % 2, 1, :], in0=psX[:], scalar=1024.0,
                                                   in1=xT[:, r % 2, 0, :], op0=ALU.mult, op1=ALU.subtract
                                                   ).then_inc(s["X_lo"], 1)
                assert not done or k[0] == LK

            def esl(n):
                return eslot[:, bass.ds(n, 1)]

            slots(dve, step)

        @block.gpsimd
        def _(pool):
            def gather(dst, src, r, sm):
                nc.gpsimd.indirect_dma_start(out=dst, out_offset=None, in_=src,
                                             in_offset=bass.IndirectOffsetOnAxis(ap=gidx[:, r % 4:r % 4 + 1], axis=0)
                                             ).then_inc(sm, 16)

            def step(n, r):
                done = within(n - 1, 0, SLOTS)
                for hc in range(HC):
                    if within(n + 1, 0, SLOTS):
                        t = (n + 1) * HC + hc
                        wait(pool, s["f_sum"], t + 1, s["apart_pool"])
                        at = a[:, (r + 1) % 2, hc, :]
                        nc.gpsimd.tensor_tensor(at, at, at, ALU.mult).then_inc(s["a_ready"], 1)
                    if hc == 2 and done:
                        wait(pool, s["o_ready"], n, s["apart_pool"])
                        rm = (r - 1) % 4
                        nc.gpsimd.indirect_dma_start(
                            out=io["out"],
                            out_offset=bass.IndirectOffsetOnAxis(ap=oidx[:, rm % 2:rm % 2 + 1], axis=0),
                            in_=ob[:], in_offset=None, bounds_check=TOK - 1, oob_is_err=False
                        ).then_inc(s["out_done"], 16)
                if done:
                    wait(pool, s["out_done"], n * 16, s["apart_pool"])
                    pool.sem_inc(s["ob_free"], 1)
                if within(n + 3, 0, SLOTS):
                    wait(pool, s["idx_ready"], n + 4, s["apart_pool"])
                    gather(xg[:, (r + 3) % 4, :], io["x"], r + 3, x_got[(r + 3) % 4])
                if within(n + 1, 0, SLOTS):
                    gather(sg[:, (r + 1) % 2, :], io["s"], r + 1, s_got[(r + 1) % 2])

            pool.sem_inc(s["ob_free"], 1)
            slots(pool, step)
            pool.wait_ge(s["out_done"], SLOTS * 16)


def build(nc, x, wqkv, bqkv, wout, bout, wr, wf, const, out):
    io = {"x": x, "wqkv": wqkv, "bqkv": bqkv, "wout": wout, "bout": bout, "wr": wr, "wf": wf,
          "const": const, "out": out,
          "s": nc.dram_tensor("attn_out", [TOK, D], F32).ap(),
          "meta": nc.dram_tensor("route", [TOK, MROW], F32).ap(),
          "qk": nc.dram_tensor("qk_parts", [2, 2, 2, P, S], F16).ap()}
    with ExitStack() as ctx:
        sc = ctx.enter_context(nc.sbuf_tensor("sc", [P, X_N], F32))
        conf = ctx.enter_context(nc.sbuf_tensor("conf", [P, C_N], F32))
        esum = ctx.enter_context(nc.sbuf_tensor("esum", [P, 1], F32))
        attention_block(nc, io, sc, conf, esum)
        ffn_block(nc, io, sc, conf, esum)


def kernel(L0_attn_x, L0_attn_Wqkv, L0_attn_b_qkv, L0_attn_Wout, L0_attn_b_out,
           L0_ffn_w_router, L0_ffn_w_fc, L0_ffn_w_proj):
    import concourse.bacc as bacc
    from concourse.bass_utils import run_bass_kernel_spmd

    def lhs(w, k):
        w = np.asarray(w)
        return np.ascontiguousarray(w.T.reshape(k, P, -1).transpose(1, 0, 2).reshape(P, -1))

    w1 = np.asarray(L0_ffn_w_fc).reshape(E, HC, 512, KC, P).transpose(0, 1, 4, 3, 2).reshape(E, HC, P, 2048)
    w2 = np.asarray(L0_ffn_w_proj).reshape(E, D, HC, 4, P).transpose(0, 2, 4, 3, 1).reshape(E, HC, P, 2048)
    arrays = {
        "x": np.ascontiguousarray(np.asarray(L0_attn_x).reshape(TOK, D)),
        "wqkv": lhs(L0_attn_Wqkv, KC),
        "bqkv": np.ascontiguousarray(np.asarray(L0_attn_b_qkv).reshape(3 * NG, P).T),
        "wout": lhs(L0_attn_Wout, NG),
        "bout": np.ascontiguousarray(np.broadcast_to(np.asarray(L0_attn_b_out), (P, D))),
        "wr": lhs(L0_ffn_w_router, KC),
        "wf": np.ascontiguousarray(np.stack([w1, w2], 2).reshape(E * HC * 2, P, 2048)),
        "const": constants(),
    }
    nc = bacc.Bacc("TRN2", target_bir_lowering=False, num_devices=1)
    args = [nc.dram_tensor("in_" + n, a.shape, mybir.dt.from_np(a.dtype), kind="ExternalInput").ap()
            for n, a in arrays.items()]
    args.append(nc.dram_tensor("out_x", (TOK, D), F32, kind="ExternalOutput").ap())
    build(nc, *args)
    r = run_bass_kernel_spmd(nc, [{"in_" + n: a for n, a in arrays.items()}], core_ids=[0])
    return r.results[0]["out_x"].reshape(B, S, D)
```

```python
import concourse.bass as bass
from concourse import mybir
from concourse.alu_op_type import AluOpType as ALU
from contextlib import ExitStack
import numpy as np

P = 128
B, S, D = 8, 512, 512
H, HD = 16, 32
TOK = B * S
KC = D // P
QB = S // P
HG = P // HD
NG = H // HG
NU = B * NG
E, HID = 2, 2048
HC = HID // 512
SLOTS = TOK // P + 1
MROW = 8
MASK = -float(2 ** 40)
OOB = 8192

ROWOFF = [P * i * (i + 1) // 2 for i in range(QB)]
CAUSAL = P * QB * (QB + 1) // 2
SEG = {0: 0, 1: 512, 3: 896, 2: 1024}
TJOBS = [[0], [1, 3], [2]]

F32, F16, I32 = mybir.dt.float32, mybir.dt.float16, mybir.dt.int32
ACT = mybir.ActivationFunctionType
AX = mybir.AxisListType
RMAX = bass.bass_isa.ReduceOp.max

C_ID, C_LT, C_BASE, C_F, C_TOK, C_NSL, C_SLOT = 0, 128, 256, 768, 772, 776, 792
C_N = C_SLOT + SLOTS
(X_SWQ, X_SWO, X_SWR, X_CK, X_CC, X_CS, X_CR, X_PA, X_PM, X_PAO, X_PAR, X_RPM, X_T0, X_T1,
 X_S1, X_S2, X_CY, X_PA1, X_PA2, X_N) = range(20)


def constants():
    c = np.zeros((P, C_N), np.float32)
    p = np.arange(P)
    c[:, C_ID:C_ID + P] = np.eye(P)
    c[:, C_LT:C_LT + P] = p[:, None] < p[None, :]
    k = np.arange(S)
    c[:, C_BASE:C_BASE + S] = k[None, :] - (S - 1)
    c[:, C_BASE + S - P:C_BASE + S] += np.where(p[None, :] > p[:, None], MASK, 0.0)
    slope = 2.0 ** (-(np.arange(H) + 1) * 8.0 / H)
    for g in range(NG):
        c[:, C_F + g] = (HD ** -0.5) / slope[g * HG + p // HD]
    for i in range(QB):
        c[:, C_TOK + i] = i * P + p
    c[:, C_NSL:C_NSL + H] = -slope[None, :]
    c[:, C_SLOT:C_SLOT + SLOTS] = P * np.arange(SLOTS)[None, :]
    return c


def wait(eng, sem, value, apart=None):
    if isinstance(value, int) and value <= 0:
        return
    eng.wait_ge(sem, value)
    if apart is not None and not isinstance(value, int):
        eng.sem_inc(apart, 1)


def within(n, lo, hi):
    return not isinstance(n, int) or lo <= n < hi


def batches(eng, iteration):
    iteration(-1, 1)
    iteration(0, 0)
    with eng.Fori(0, (B - 2) // 2) as it:
        iteration(it * 2 + 1, 1)
        iteration(it * 2 + 2, 0)
    iteration(B - 1, 1)
    iteration(B, 0)


JOBS = [("q", 0, 2), ("k", 0, 2), ("q", 0, 3), ("k", 0, 3),
        ("o", -1, 0), ("x", 1, 0), ("o", -1, 1), ("x", 1, 1),
        ("o", -1, 2), ("x", 1, 2), ("o", -1, 3), ("x", 1, 3),
        ("q", 1, 0), ("k", 1, 0), ("v", 1, 0), ("logits", 1, 0), ("v", 1, 1),
        ("q", 1, 1), ("k", 1, 1), ("rank", 1, 0), ("v", 1, 2), ("v", 1, 3)]
STEP = [(0,), (1,), (2,), (3,), (4, 5), (6, 7), (8, 9), (10, 11),
        (12,), (13,), (14, 15), (16,), (17,), (18, 19), (20,), (21,)]
NJOB = len(JOBS)
ABANKS = 2
S_LEAD, M_LEAD, E_LEAD, N_LEAD = 4, 3, 2, 1


def job_exists(b, pos):
    return not isinstance(b, int) or 0 <= b + JOBS[pos][1] < B


def head_at(b, n):
    return (b, n) if 0 <= n < H else ((b + 1, n - H) if n >= H else (b - 1, n + H))


def attention_block(nc, io, sc, conf, esum):
    with ExitStack() as ctx:
        sb = lambda n, s, d: ctx.enter_context(nc.sbuf_tensor(n, s, d))
        sem = lambda n: ctx.enter_context(nc.semaphore(n))
        wqkv = sb("wqkv", [P, KC, 2, 3 * D], F16)
        wout = sb("wout", [P, NG, 2, D], F16)
        wr = sb("wr", [P, KC, 2, E], F16)
        wr_f = sb("wr_f", [P, KC * E], F32)
        bqk = sb("bqk", [P, 3 * NG], F32)
        bqs = sb("bqs", [P, 3 * NG], F32)
        cq = sb("cq", [P, NG], F32)
        nsl = sb("nsl", [P, H], F32)
        base = sb("base", [P, S], F32)
        bout = sb("bout", [P, D], F32)
        lt16 = sb("lt16", [P, P], F16)
        ones16 = sb("ones16", [P, P], F16)
        tid = sb("tid", [P, QB], F32)
        am = sb("am", [P, 8], F32)
        amr = sb("amr", [P, 8], F32)
        fam = sb("fam", [P, 4], F32)
        xin = sb("xin", [P, QB, D], F32)
        xn = sb("xn", [P, QB, D], F32)
        stat = sb("stat", [P, QB, 6], F32)
        mv = sb("mv", [P, QB, 2], F32)
        veps = sb("veps", [P, QB], F32)
        half = sb("half", [P, QB], F32)
        rstd = sb("rstd", [P, 2, QB], F32)
        xT = sb("xT", [P, 2, 2, KC, S], F16)
        stage = sb("stage", [P, 2, S], F32)
        pre = sb("pre", [P, 2, 2, S], F16)
        qs = sb("qs", [P, 2, HG, S], F16)
        ks = sb("ks", [P, 2, HG, S], F16)
        v = sb("v", [P, 2, 2, QB, D], F16)
        pr = sb("pr", [P, HG, CAUSAL], F32)
        mn = sb("mn", [P, HG * QB], F32)
        den = sb("den", [P, HG * QB], F32)
        rden = sb("rden", [P, HG * QB], F32)
        pt = sb("pt", [P, 2, 2, HG, CAUSAL], F16)
        cf = sb("cf", [P, S], F32)
        cx = sb("cx", [P, NG, 2, S], F16)
        so = sb("so", [P, QB, D], F32)
        wst = sb("wst", [P, 2048], F32)
        lg = sb("lg", [P, QB, E], F32)
        dl = sb("dl", [P, QB], F32)
        nd = sb("nd", [P, QB], F32)
        ex = sb("ex", [P, QB], F32)
        e16 = sb("e16", [P, QB + 1], F16)
        epre = sb("epre", [P, QB + 1], F16)
        ef = sb("ef", [P, QB + 1], F32)
        rk = sb("rk", [P, QB + 1], F32)
        t0 = sb("t0", [P, QB], F32)
        t1 = sb("t1", [P, QB], F32)
        pos = sb("pos", [P, QB], I32)
        meta = sb("meta", [P, QB, MROW], F32)

        psA = [ctx.enter_context(nc.psum_tensor(f"psA{i}", [P, 512], F32)) for i in range(ABANKS)]
        psS = [ctx.enter_context(nc.psum_tensor(f"psS{i}", [P, 512], F32)) for i in range(3)]
        rows = [psS[0][:, 0:P], psS[0][:, P:3 * P], psS[1][:, 0:3 * P], psS[2][:, 0:4 * P]]
        psT = [ctx.enter_context(nc.psum_tensor(f"psT{i}", [P, 512], F32)) for i in range(2)]
        psC = ctx.enter_context(nc.psum_tensor("psC", [P, 512], F32))

        names = ("const_in w_in wr_in absmax allmax scales w_split_hi w_split_lo setup consts_made "
                 "ln_stats rstd_ready xn_ready xT_done xT_hi xT_lo V_done V_hi V_lo "
                 "qk_done qk_staged qk_hi qk_lo S_done ttr_done exp_done rden_done norm_done "
                 "T_done T_hi T_lo PV_done ctx_staged ctx_hi ctx_lo O_done O_evac "
                 "R_done R_part R2_done logits_read rank_read e_ready nd_ready rexp_done meta_ready wmax_in wmax_done "
                 "apart_dve apart_sp apart_pool dve_link wm_link pool_link meta_out").split()
        s = {n: sem(n) for n in names}
        x_in = [sem(f"x_in{i}") for i in range(QB)]
        s_out = [sem(f"s_out{i}") for i in range(QB)]
        stored = [sem("q_stored"), sem("k_stored")]
        stacked = [[sem(f"{n}_stacked{p}") for p in range(2)] for n in "qk"]

        wflat = pt[:, :, :, :, :].rearrange("p a b h n -> p (a b h n)").bitcast(F32)
        wq_f = wflat[:, 0:KC * 3 * D]
        wo_f = wflat[:, KC * 3 * D:KC * 3 * D + NG * D]

        def job_count(b, p):
            kind, db, i = JOBS[p]
            if kind in ("logits", "rank"):
                return s[kind + "_read"], b + db + 1
            n = (b + db) * QB + i
            if kind in ("q", "k"):
                return s["qk_staged"], n * 2 + 1 + (kind == "k")
            return s[{"o": "O_evac", "x": "xT_lo", "v": "V_lo"}[kind]], n + 1

        def jobs_before(b, odd, step):
            b, odd, step = (b, odd, step - 1) if step else (b - 1, 1 - odd, len(STEP) - 1)
            for p in STEP[step]:
                kind, db, i = JOBS[p]
                if job_exists(b, p):
                    yield kind, b + db, i, (odd + db) % 2, psA[p % ABANKS]

        block = ctx.enter_context(nc.Block())

        @block.sync
        def _(sp):
            for i in range(QB):
                sp.sem_inc(s_out[i], 16)
            sp.dma_start(conf[:], io["const"]).then_inc(s["const_in"], 16)
            for i in range(QB):
                sp.dma_start(xin[:, i, :], io["x"][i * P:(i + 1) * P, :]).then_inc(x_in[i], 16)
            sp.dma_start(wq_f, io["wqkv"]).then_inc(s["w_in"], 16)
            sp.dma_start(wo_f, io["wout"]).then_inc(s["w_in"], 16)
            sp.dma_start(wr_f[:], io["wr"]).then_inc(s["wr_in"], 16)
            sp.dma_start(bqk[:], io["bqkv"]).then_inc(s["wr_in"], 16)
            sp.dma_start(bout[:], io["bout"]).then_inc(s["wr_in"], 16)

            def stack(b, g):
                u = b * NG + g
                if not within(u, 0, NU):
                    return
                par = g % 2
                for w, dst, parts in ((0, qs, (0, 1, 0, 1)), (1, ks, (0, 0, 1, 1))):
                    wait(sp, s["qk_hi"], u * 2 + 1 + w, s["apart_sp"])
                    wait(sp, s["qk_lo"], u * 2 + 1 + w, s["apart_sp"])
                    wait(sp, stacked[w][par], (b * 2 + g // 2) * 64, s["apart_sp"])
                    sp.dma_start(io["qk"][w, par].rearrange("a p n -> p a n"),
                                 pre[:, w, :, :]).then_inc(stored[w], 16)
                    wait(sp, stored[w], (u + 1) * 16, s["apart_sp"])
                    wait(sp, s["S_done"], (u - 1) * 16, s["apart_sp"])
                    for r in range(4):
                        sp.dma_start(dst[r * HD:(r + 1) * HD, par, :, :],
                                     io["qk"][w, par, parts[r]].rearrange("(j d) n -> d j n", j=HG)
                                     ).then_inc(stacked[w][par], 16)

            def iteration(b, odd):
                if within(b, 0, B - 1):
                    for i in range(QB):
                        wait(sp, s["xn_ready"], b * QB + i + 1, s["apart_sp"])
                        sp.dma_start(xin[:, i, :], io["x"][bass.ds((b + 1) * S + i * P, P), :]
                                     ).then_inc(x_in[i], 16)
                if within(b, 0, B):
                    wait(sp, s["wmax_done"], b * 4, s["apart_sp"])
                    sp.dma_start(wst[:], io["wf"][bass.ds(b * 2, 1)].rearrange("o p n -> (o p) n")
                                 ).then_inc(s["wmax_in"], 16)
                    stack(b, 2)
                if within(b, 0, B):
                    stack(b, 3)
                if within(b, 1, B + 1):
                    for i in range(QB):
                        wait(sp, s["O_evac"], (b - 1) * QB + i + 1, s["apart_sp"])
                        sp.dma_start(io["s"][bass.ds((b - 1) * S + i * P, P), :], so[:, i, :]
                                     ).then_inc(s_out[i], 16)
                if within(b, 0, B):
                    wait(sp, s["wmax_done"], b * 4 + 2, s["apart_sp"])
                    sp.dma_start(wst[:], io["wf"][bass.ds(b * 2 + 1, 1)].rearrange("o p n -> (o p) n")
                                 ).then_inc(s["wmax_in"], 16)
                if within(b, -1, B - 1):
                    stack(b + 1, 0)
                    stack(b + 1, 1)

            batches(sp, iteration)
            for i in range(QB):
                sp.wait_ge(s_out[i], 16 * (B + 1))

        @block.tensor
        def _(pe):
            def bank(b, p):
                bb, q = b, p - ABANKS
                while True:
                    if q < 0:
                        bb, q = bb - 1, q + NJOB
                    if isinstance(bb, int) and bb < -1:
                        break
                    if job_exists(bb, q):
                        if JOBS[p] != ("q", 1, 0):
                            wait(pe, *job_count(bb, q))
                        break
                    q -= ABANKS
                return psA[p % ABANKS]

            def products(ps, pairs, mid, done):
                for n, (a, x) in enumerate(pairs):
                    if n == len(pairs) // 2:
                        mid()
                    last = nc.tensor.matmul(ps, a, x, start=(n == 0), stop=(n == len(pairs) - 1))
                last.then_inc(done, 1)

            PARTS = ((0, 0), (1, 0), (0, 1))

            def job(b, odd, p, mid):
                kind, db, i = JOBS[p]
                batch, par = b + db, (odd + db) % 2
                if kind in ("q", "k"):
                    if (kind, db, i) == ("q", 1, 0):
                        wait(pe, s["xT_lo"], (batch + 1) * QB)
                    ps = bank(b, p)
                    col = (kind == "k") * D + i * P
                    products(ps[:], [(wqkv[:, kc, a, col:col + P], xT[:, par, x, kc, :])
                                     for x, a in PARTS for kc in range(KC)], mid, s["qk_done"])
                elif kind == "v":
                    ps = bank(b, p)
                    products(ps[:], [(xT[:, par, x, kc, i * P:(i + 1) * P], wqkv[:, kc, a, 2 * D:3 * D])
                                     for x, a in PARTS for kc in range(KC)], mid, s["V_done"])
                elif kind == "o":
                    ps = bank(b, p)
                    if i == 0:
                        wait(pe, s["ctx_hi"], (batch + 1) * NG)
                        wait(pe, s["ctx_lo"], (batch + 1) * NG)
                    products(ps[:], [(cx[:, g, x, i * P:(i + 1) * P], wout[:, g, a, :])
                                     for x, a in PARTS for g in range(NG)], mid, s["O_done"])
                elif kind == "logits":
                    ps = bank(b, p)
                    for t in range(QB):
                        products(ps[:, t * E:(t + 1) * E],
                                 [(xT[:, par, x, kc, t * P:(t + 1) * P], wr[:, kc, a, :])
                                  for x, a in PARTS for kc in range(KC)], mid,
                                 s["R_done"] if t == QB - 1 else s["R_part"])
                elif kind == "rank":
                    ps = bank(b, p)
                    wait(pe, s["e_ready"], batch + 1)
                    nc.tensor.matmul(ps[:, 0:QB + 1], lt16[:], e16[:], start=True, stop=False)
                    nc.tensor.matmul(ps[:, 0:QB + 1], ones16[:], epre[:], start=False, stop=True
                                     ).then_inc(s["R2_done"], 1)
                else:
                    ps = bank(b, p)
                    mid()
                    wait(pe, s["xn_ready"], batch * QB + i + 1)
                    for kc in range(KC):
                        last = nc.tensor.transpose(ps[:, kc * P:(kc + 1) * P], xn[:, i, kc * P:(kc + 1) * P],
                                                   conf[:, C_ID:C_ID + P])
                    last.then_inc(s["xT_done"], 1)

            def scores(b, h):
                g, j = h // HG, h % HG
                par = g % 2
                n = (b * H + h) * QB
                if j == 0:
                    for w in range(2):
                        wait(pe, stacked[w][par], (b * 2 + g // 2 + 1) * 64)
                for i in range(QB):
                    if i != 1:
                        wait(pe, s["ttr_done"], n - QB + max(i, 1) + 1)
                    nc.tensor.matmul(rows[i], qs[:, par, j, i * P:(i + 1) * P],
                                     ks[:, par, j, 0:(i + 1) * P], start=True, stop=True
                                     ).then_inc(s["S_done"], 1)

            def ptrans(b, g, j, r):
                if not within(b, 0, B):
                    return
                h = b * H + g * HG + j
                if r == 0:
                    wait(pe, s["norm_done"], (h + 1) * QB)
                ps = psT[(3 * j + r) % 2]
                wait(pe, s["T_lo"], h * 3 + r - 1)
                kbs = TJOBS[r]
                for kb in kbs:
                    for i in range(kb, QB):
                        o = SEG[kb] - SEG[kbs[0]] + (i - kb) * P
                        c = ROWOFF[i] + kb * P
                        last = nc.tensor.transpose(ps[:, o:o + P], pr[:, j, c:c + P],
                                                   conf[:, C_ID:C_ID + P])
                last.then_inc(s["T_done"], 1)

            def pv(b, g, par):
                u = b * NG + g
                wait(pe, s["T_lo"], (u + 1) * 12)
                if g == 0:
                    wait(pe, s["V_lo"], (b + 1) * QB)
                wait(pe, s["ctx_staged"], u)
                for kb in range(QB):
                    w = S - kb * P
                    for n, (x, a) in enumerate(((0, 0), (0, 1), (1, 0))):
                        for j in range(HG):
                            c = (g * HG + j) * HD
                            last = nc.tensor.matmul(
                                psC[j * HD:(j + 1) * HD, kb * P:S], v[:, par, a, kb, c:c + HD],
                                pt[:, g % 2, x, j, SEG[kb]:SEG[kb] + w],
                                start=(kb == 0 and n == 0), stop=(kb == QB - 1 and n == 2))
                last.then_inc(s["PV_done"], 1)

            def iteration(b, odd):
                for step in range(H):
                    g, j = step // HG, step % HG
                    ptrans(b, g, j, 0)
                    todo = [p for p in STEP[step] if job_exists(b, p)]

                    def between():
                        ptrans(b, g, j, 1)

                    if not todo:
                        between()
                    for n, p in enumerate(todo):
                        job(b, odd, p, between if n == 0 else lambda: None)
                    ptrans(b, g, j, 2)
                    hb, h = head_at(b, step + S_LEAD)
                    if within(hb, 0, B):
                        scores(hb, h)
                    if j == 0:
                        pb, pg = (b, g - 1) if g else (b - 1, NG - 1)
                        if within(pb, 0, B):
                            pv(pb, pg, odd if g else 1 - odd)

            pe.sem_inc(s["O_done"], 1)
            pe.wait_ge(s["consts_made"], 1)
            pe.wait_ge(s["w_split_hi"], 3)
            pe.wait_ge(s["w_split_lo"], 3)
            batches(pe, iteration)

        @block.scalar
        def _(act):
            act.wait_ge(s["scales"], 1)
            for dst, src, c in ((wqkv, wq_f, X_SWQ), (wout, wo_f, X_SWO), (wr, wr_f[:, :], X_SWR)):
                n = dst.shape[3]
                nc.scalar.activation(dst[:, :, 0, :], src.rearrange("p (k n) -> p k n", n=n), ACT.Copy,
                                     scale=sc[:, c:c + 1]).then_inc(s["w_split_hi"], 1)

            def read_out(kind, b, i, par, ps):
                if kind in ("q", "k"):
                    w, n = int(kind == "k"), (b * NG + i) * 2
                    wait(act, s["qk_done"], n + 1 + w)
                    wait(act, s["qk_lo"], n - 1 + w)
                    nc.scalar.activation(stage[:, w, :], ps[:], ACT.Identity,
                                         bias=bqs[:, w * NG + i:w * NG + i + 1],
                                         scale=cq[:, i:i + 1] if w == 0 else sc[:, X_CK:X_CK + 1]
                                         ).then_inc(s["qk_staged"], 1)
                elif kind == "x":
                    if i == 0:
                        wait(act, s["V_done"], (b - 1) * QB)
                        wait(act, s["qk_done"], (b - 1) * 2 * NG)
                        wait(act, s["R_done"], b - 1)
                    wait(act, s["xT_done"], b * QB + i + 1)
                    nc.scalar.activation(xT[:, par, 0, :, i * P:(i + 1) * P],
                                         ps[:].rearrange("p (k n) -> p k n", k=KC),
                                         ACT.Copy, scale=1024.0).then_inc(s["xT_hi"], 1)
                elif kind == "v":
                    wait(act, s["V_done"], b * QB + i + 1)
                    if i == 0:
                        wait(act, s["PV_done"], (b - 1) * NG)
                    nc.scalar.activation(v[:, par, 0, i, :], ps[:], ACT.Copy,
                                         scale=2.0 ** -19).then_inc(s["V_hi"], 1)

            def iteration(b, odd):
                more = within(b, -1, B - 1)
                for step in range(H):
                    g, j = step // HG, step % HG
                    hd = b * H + step
                    hb, h = head_at(b, step + E_LEAD)

                    def high(r):
                        if not within(b, 0, B):
                            return
                        kbs = TJOBS[r]
                        w = sum(S - kb * P for kb in kbs)
                        o = SEG[kbs[0]]
                        if r == 0 and j == 0:
                            wait(act, s["PV_done"], b * NG + g - 1)
                        wait(act, s["T_done"], hd * 3 + r + 1)
                        nc.scalar.activation(pt[:, g % 2, 0, j, o:o + w],
                                             psT[(3 * j + r) % 2][:, 0:w], ACT.Copy
                                             ).then_inc(s["T_hi"], 1)

                    def exps(i):
                        if not within(hb, 0, B):
                            return
                        c = (h % HG) * QB + i
                        if i == 0:
                            wait(act, s["rden_done"], hb * H + h - HG + 1)
                        wait(act, s["ttr_done"], (hb * H + h) * QB + i + 1)
                        p_ = pr[:, h % HG, ROWOFF[i]:ROWOFF[i] + (i + 1) * P]
                        nc.scalar.activation(p_, p_, ACT.Exp, bias=mn[:, c:c + 1], scale=-1.0,
                                             accum_out=den[:, c:c + 1]).then_inc(s["exp_done"], 1)

                    for args in jobs_before(b, odd, step):
                        read_out(*args)
                    high(0)
                    if j == 1:
                        pb, pg = (b, g - 1) if g else (b - 1, NG - 1)
                        if within(pb, 0, B):
                            u = pb * NG + pg
                            wait(act, s["PV_done"], u + 1)
                            wait(act, s["ctx_lo"], u)
                            nc.scalar.activation(cf[:], psC[:], ACT.Identity,
                                                 bias=bqs[:, 2 * NG + pg:2 * NG + pg + 1],
                                                 scale=sc[:, X_CC:X_CC + 1]).then_inc(s["ctx_staged"], 1)
                    exps(0)
                    exps(1)
                    exps(2)
                    high(1)
                    exps(3)
                    high(2)
                    if more and step == 12:
                        wait(act, s["nd_ready"], b + 2)
                        nc.scalar.activation(ex[:], nd[:], ACT.Exp).then_inc(s["rexp_done"], 1)

            batches(act, iteration)

        @block.vector
        def _(dve):
            n_setup = [0]

            def setup(ins):
                n_setup[0] += 1
                ins.then_inc(s["setup"], 1)
                dve.wait_ge(s["setup"], n_setup[0])

            dve.wait_ge(s["const_in"], 16)
            nc.vector.memset(half[:], -0.5)
            nc.vector.memset(esum[:], 0.0)
            nc.vector.memset(fam[:], 0.0)
            nc.vector.memset(ones16[:], 1.0)
            nc.vector.memset(e16[:], 0.0)
            nc.vector.memset(epre[:], 0.0)
            nc.vector.memset(am[:], 0.0)
            nc.vector.memset(meta[:], 0.0)
            nc.vector.tensor_copy(tid[:], conf[:, C_TOK:C_TOK + QB])
            setup(nc.vector.tensor_copy(lt16[:], conf[:, C_LT:C_LT + P]))
            n_setup[0] += 1
            nc.vector.memset(t0[:], 0.0).then_inc(s["setup"], 1)
            dve.wait_ge(s["setup"], n_setup[0])

            dve.wait_ge(s["w_in"], 32)
            dve.wait_ge(s["wr_in"], 48)
            for c, src in ((0, wq_f), (1, bqk[:, :]), (2, wo_f), (3, wr_f[:, :])):
                setup(nc.vector.tensor_reduce(am[:, c:c + 1], src, AX.X, ALU.max, apply_absolute_value=True))
            nc.vector.tensor_scalar(am[:, 0:4], am[:, 0:4], 1.0, None, ALU.mult).then_inc(s["absmax"], 1)
            dve.wait_ge(s["allmax"], 1)
            x = lambda c, n=1: sc[:, c:c + n]

            def pow2(dst, src):
                setup(nc.vector.tensor_scalar(dst.bitcast(I32), src.bitcast(I32), 0x7F800000, None,
                                              ALU.bitwise_and))

            ts = nc.vector.tensor_scalar
            setup(ts(amr[:, 0:4], amr[:, 0:4], 1e-9, None, ALU.max))
            setup(ts(x(X_T0), amr[:, 0:1], float(D), amr[:, 1:2], ALU.mult, ALU.add))
            pow2(x(X_PA), amr[:, 0:1])
            pow2(x(X_PM), x(X_T0))
            pow2(x(X_PAO), amr[:, 2:3])
            pow2(x(X_PAR), amr[:, 3:4])
            for dst, src in ((X_SWQ, X_PA), (X_SWO, X_PAO), (X_SWR, X_PAR), (X_RPM, X_PM)):
                setup(nc.vector.reciprocal(x(dst), x(src)))
            setup(ts(x(X_SWQ, 3), x(X_SWQ, 3), 2.0 ** 14, None, ALU.mult))
            setup(ts(x(X_T1), x(X_RPM), x(X_PA), None, ALU.mult))
            setup(ts(x(X_CK), x(X_T1), 2.0 ** -10, None, ALU.mult))
            setup(ts(x(X_CC), x(X_T1), 2.0 ** -6, None, ALU.mult))
            setup(nc.vector.tensor_tensor(x(X_CS), x(X_PM), x(X_PAO), ALU.mult))
            setup(ts(x(X_CS), x(X_CS), 2.0 ** -28, None, ALU.mult))
            setup(ts(x(X_CR), x(X_PAR), 2.0 ** -24, None, ALU.mult))
            setup(ts(cq[:], conf[:, C_F:C_F + NG], x(X_T1), None, ALU.mult))
            setup(ts(cq[:], cq[:], 2.0 ** -16, None, ALU.mult))
            setup(ts(bqs[:], bqk[:], x(X_RPM), None, ALU.mult))
            setup(ts(bqs[:], bqs[:], 2.0 ** 14, None, ALU.mult))
            setup(nc.vector.tensor_tensor(bqs[:, 0:NG], bqs[:, 0:NG], conf[:, C_F:C_F + NG], ALU.mult))
            setup(ts(bqs[:, 0:NG], bqs[:, 0:NG], 2.0 ** -6, None, ALU.mult))
            setup(nc.vector.tensor_tensor(x(X_T0), x(X_PM), x(X_PM), ALU.mult))
            setup(ts(x(X_T0), x(X_T0), 2.0 ** -22, None, ALU.mult))
            setup(ts(nsl[:], conf[:, C_NSL:C_NSL + H], x(X_T0), None, ALU.mult))
            setup(nc.vector.reciprocal(x(X_T0), x(X_T0)))
            setup(ts(base[:], conf[:, C_BASE:C_BASE + S], x(X_T0), None, ALU.mult))
            nc.vector.memset(t1[:], 0.0).then_inc(s["scales"], 1)
            for n, (dst, src, c) in enumerate(((wqkv, wq_f, X_SWQ), (wout, wo_f, X_SWO), (wr, wr_f[:, :], X_SWR))):
                dve.wait_ge(s["w_split_hi"], n + 1)
                w3 = src.rearrange("p (k n) -> p k n", n=dst.shape[3])
                nc.vector.scalar_tensor_tensor(out=dst[:, :, 1, :], in0=w3, scalar=x(c), in1=dst[:, :, 0, :],
                                               op0=ALU.mult, op1=ALU.subtract).then_inc(s["w_split_lo"], 1)
            nc.vector.memset(t1[:], 0.0).then_inc(s["consts_made"], 1)

            WMAX_AT = (4, 8, 12, 15)
            LINKS = 17

            def iteration(b, odd):
                nxt, par = b + 1, 1 - odd
                more = within(b, -1, B - 1)
                k = [0]

                def link(ins):
                    k[0] += 1
                    ins.then_inc(s["dve_link"], 1)
                    wait(dve, s["dve_link"], (b + 1) * LINKS + k[0], s["apart_dve"])

                def ln_stats(i):
                    wait(dve, x_in[i], (nxt + 1) * 16)
                    link(nc.vector.bn_stats(stat[:, i, :], xin[:, i, :]))
                    nc.vector.bn_aggr(mv[:, i, :], stat[:, i, :]).then_inc(s["ln_stats"], 1)

                def ln_apply(i):
                    if i == 0:
                        wait(dve, s["rstd_ready"], nxt + 1)
                    wait(dve, s["xT_done"], b * QB + i + 1)
                    nc.vector.tensor_scalar(xn[:, i, :], xin[:, i, :], mv[:, i, 0:1], rstd[:, par, i:i + 1],
                                            ALU.subtract, ALU.mult).then_inc(s["xn_ready"], 1)

                def read_out(kind, bj, i, pj, ps):
                    if kind == "x":
                        wait(dve, s["xT_hi"], bj * QB + i + 1)
                        nc.vector.scalar_tensor_tensor(
                            out=xT[:, pj, 1, :, i * P:(i + 1) * P],
                            in0=ps[:].rearrange("p (k n) -> p k n", k=KC), scalar=1024.0,
                            in1=xT[:, pj, 0, :, i * P:(i + 1) * P], op0=ALU.mult, op1=ALU.subtract
                        ).then_inc(s["xT_lo"], 1)
                    elif kind == "v":
                        wait(dve, s["V_hi"], bj * QB + i + 1)
                        nc.vector.scalar_tensor_tensor(
                            out=v[:, pj, 1, i, :], in0=ps[:], scalar=2.0 ** -19,
                            in1=v[:, pj, 0, i, :], op0=ALU.mult, op1=ALU.subtract).then_inc(s["V_lo"], 1)
                    elif kind == "o":
                        wait(dve, s["O_done"], bj * QB + i + 2)
                        wait(dve, s_out[i], (bj + 1) * 16)
                        nc.vector.scalar_tensor_tensor(
                            out=so[:, i, :], in0=ps[:], scalar=x(X_CS),
                            in1=bout[:], op0=ALU.mult, op1=ALU.add).then_inc(s["O_evac"], 1)
                    elif kind == "logits":
                        choose(ps[:, 0:QB * E])
                    elif kind == "rank":
                        place(ps[:, 0:QB + 1])
                    else:
                        w, n = int(kind == "k"), (bj * NG + i) * 2
                        wait(dve, s["qk_staged"], n + 1 + w)
                        wait(dve, stored[w], (bj * NG + i) * 16)
                        nc.vector.tensor_copy(pre[:, w, 0, :], stage[:, w, :]).then_inc(s["qk_hi"], 1)

                def choose(psR):
                    wait(dve, s["R_done"], nxt + 1)
                    wait(dve, s["R2_done"], nxt)
                    ts(lg[:].rearrange("p i e -> p (i e)"), psR, x(X_CR), None, ALU.mult
                       ).then_inc(s["logits_read"], 1)
                    dve.wait_ge(s["logits_read"], nxt + 1)
                    link(nc.vector.tensor_tensor(dl[:], lg[:, :, 1], lg[:, :, 0], ALU.subtract))
                    nc.vector.scalar_tensor_tensor(out=nd[:], in0=dl[:], scalar=-1.0, in1=dl[:],
                                                   op0=ALU.mult, op1=ALU.min).then_inc(s["nd_ready"], 1)
                    link(ts(ef[:, 0:QB], dl[:], 0.0, None, ALU.is_gt))
                    nc.vector.tensor_copy(e16[:, 0:QB], ef[:, 0:QB])
                    link(nc.vector.tensor_copy(epre[:, 1:2], ef[:, 0:1]))
                    for i in range(1, QB):
                        link(nc.vector.tensor_tensor(epre[:, i + 1:i + 2], epre[:, i:i + 1], ef[:, i:i + 1],
                                                     ALU.add))
                    nc.vector.memset(t0[:, 0:1], 0.0).then_inc(s["e_ready"], 1)

                def place(psK):
                    wait(dve, s["R2_done"], nxt + 1)
                    wait(dve, s["rexp_done"], nxt + 1)
                    wait(dve, s["meta_out"], nxt * QB * 16)
                    nc.vector.tensor_scalar(rk[:], psK, esum[:, 0:1], None, ALU.add
                                            ).then_inc(s["rank_read"], 1)
                    dve.wait_ge(s["rank_read"], nxt + 1)
                    nc.vector.tensor_copy(esum[:, 0:1], rk[:, QB:QB + 1])
                    link(nc.vector.tensor_tensor(t0[:], tid[:], rk[:, 0:QB], ALU.subtract))
                    link(ts(t1[:], tid[:], -1.0, float(TOK - 1), ALU.mult, ALU.add))
                    link(nc.vector.tensor_tensor(t1[:], t1[:], ef[:, 0:QB], ALU.mult))
                    link(nc.vector.tensor_tensor(t0[:], t0[:], t1[:], ALU.add))
                    nc.vector.tensor_copy(pos[:], t0[:])
                    nc.vector.tensor_copy(meta[:, :, 0], tid[:])
                    link(ts(t1[:], ex[:], 1.0, None, ALU.add))
                    nc.vector.tensor_copy(meta[:, :, 2], ef[:, 0:QB])
                    nc.vector.tensor_copy(meta[:, :, 3], mv[:, :, 0])
                    nc.vector.tensor_copy(meta[:, :, 4], rstd[:, par, :])
                    link(nc.vector.reciprocal(meta[:, :, 1], t1[:]))
                    link(ts(tid[:], tid[:], float(S), None, ALU.add))
                    nc.vector.memset(rk[:, 0:1], 0.0).then_inc(s["meta_ready"], 1)

                for step in range(H):
                    g, j = step // HG, step % HG
                    hd = b * H + step
                    hb, h = head_at(b, step + M_LEAD)

                    def low(r):
                        if not within(b, 0, B):
                            return
                        kbs = TJOBS[r]
                        w = sum(S - kb * P for kb in kbs)
                        o = SEG[kbs[0]]
                        wait(dve, s["T_hi"], hd * 3 + r + 1)
                        nc.vector.tensor_tensor(pt[:, g % 2, 1, j, o:o + w], psT[(3 * j + r) % 2][:, 0:w],
                                                pt[:, g % 2, 0, j, o:o + w], ALU.subtract
                                                ).then_inc(s["T_lo"], 1)

                    def masked(i):
                        if not within(hb, 0, B):
                            return
                        if i == 0:
                            wait(dve, s["T_done"], (hb * H + h - HG + 1) * 3)
                        w = (i + 1) * P
                        c = (h % HG) * QB + i
                        wait(dve, s["S_done"], (hb * H + h) * QB + max(i, 1) + 1, s["apart_dve"])
                        nc.vector.tensor_tensor_reduce(
                            out=pr[:, h % HG, ROWOFF[i]:ROWOFF[i] + w], in0=rows[i],
                            in1=base[:, S - w:S], scale=nsl[:, h:h + 1], scalar=3e38,
                            op0=ALU.add, op1=ALU.min, accum_out=mn[:, c:c + 1]).then_inc(s["ttr_done"], 1)

                    rb, rh = head_at(b, step + N_LEAD)
                    if within(rb, 0, B):
                        wait(dve, s["exp_done"], (rb * H + rh + 1) * QB)
                        wait(dve, s["norm_done"], (rb * H + rh - HG + 1) * QB)
                        c = (rh % HG) * QB
                        nc.vector.reciprocal(rden[:, c:c + QB], den[:, c:c + QB]).then_inc(s["rden_done"], 1)
                    late = []
                    for args in jobs_before(b, odd, step):
                        if args[0] in ("q", "k"):
                            late.append(args)
                        else:
                            read_out(*args)
                    masked(0)
                    masked(1)
                    low(0)
                    masked(2)
                    masked(3)
                    low(1)
                    for args in late:
                        read_out(*args)
                    low(2)
                    if more:
                        if step < 2:
                            ln_stats(2 * step)
                            ln_stats(2 * step + 1)
                        elif step < 4:
                            ln_apply(2 * step - 4)
                            ln_apply(2 * step - 3)
                    if within(b, 0, B) and step in WMAX_AT:
                        m = WMAX_AT.index(step)
                        c, lo = m // 2, m % 2 * (2048 // 2)
                        wait(dve, s["wmax_in"], (b * 2 + c + 1) * 16)
                        nc.vector.tensor_reduce(fam[:, 2:3], wst[:, lo:lo + 2048 // 2], AX.X, ALU.max,
                                                apply_absolute_value=True).then_inc(s["wmax_done"], 1)
                        dve.wait_ge(s["wmax_done"], b * 4 + m + 1)
                        nc.vector.tensor_tensor(fam[:, c:c + 1], fam[:, c:c + 1], fam[:, 2:3], ALU.max
                                                ).then_inc(s["wm_link"], 1)
                        dve.wait_ge(s["wm_link"], b * 4 + m + 1)
                    if j == (3 if g else 2):
                        pb, pg = (b, g - 1) if g else (b - 1, NG - 1)
                        if within(pb, 0, B):
                            wait(dve, s["ctx_staged"], pb * NG + pg + 1)
                            wait(dve, s["O_done"], pb * QB + 1)
                            nc.vector.tensor_copy(cx[:, pg, 0, :], cf[:]).then_inc(s["ctx_hi"], 1)
                assert not more or k[0] == LINKS, k[0]

            batches(dve, iteration)

        @block.gpsimd
        def _(pool):
            pool.wait_ge(s["absmax"], 1)
            nc.gpsimd.partition_all_reduce(amr[:, 0:4], am[:, 0:4], P, RMAX).then_inc(s["allmax"], 1)

            def iteration(b, odd):
                nxt, par = b + 1, 1 - odd
                more = within(b, -1, B - 1)
                for step in range(H):
                    g, j = step // HG, step % HG
                    rb, rh = head_at(b, step + N_LEAD)
                    if within(rb, 0, B):
                        wait(pool, s["rden_done"], rb * H + rh + 1, s["apart_pool"])
                        for i in range(QB):
                            c = (rh % HG) * QB + i
                            p_ = pr[:, rh % HG, ROWOFF[i]:ROWOFF[i] + (i + 1) * P]
                            nc.gpsimd.tensor_scalar(p_, p_, rden[:, c:c + 1], 32768.0, ALU.mult, ALU.mult
                                                    ).then_inc(s["norm_done"], 1)
                    for kind, bj, i, _, _ in jobs_before(b, odd, step):
                        if kind in ("q", "k"):
                            w = int(kind == "k")
                            wait(pool, s["qk_hi"], (bj * NG + i) * 2 + 1 + w, s["apart_pool"])
                            nc.gpsimd.tensor_tensor(pre[:, w, 1, :], stage[:, w, :], pre[:, w, 0, :],
                                                    ALU.subtract).then_inc(s["qk_lo"], 1)
                    if more and step == 1:
                        wait(pool, s["ln_stats"], (nxt + 1) * QB, s["apart_pool"])
                        wait(pool, s["meta_ready"], nxt - 1, s["apart_pool"])
                        nc.gpsimd.tensor_scalar(veps[:], mv[:, :, 1], 1e-5, 1.0, ALU.add, ALU.mult
                                                ).then_inc(s["pool_link"], 1)
                        wait(pool, s["pool_link"], nxt + 1, s["apart_pool"])
                        nc.gpsimd.tensor_tensor(rstd[:, par, :], veps[:], half[:], ALU.pow
                                                ).then_inc(s["rstd_ready"], 1)
                    pb, pg = (b, g - 1) if g else (b - 1, NG - 1)
                    if j == (3 if g else 2) and within(pb, 0, B):
                        wait(pool, s["ctx_hi"], pb * NG + pg + 1, s["apart_pool"])
                        nc.gpsimd.tensor_tensor(cx[:, pg, 1, :], cf[:], cx[:, pg, 0, :], ALU.subtract
                                                ).then_inc(s["ctx_lo"], 1)
                    if more and step == 15:
                        wait(pool, s["meta_ready"], nxt + 1, s["apart_pool"])
                        for i in range(QB):
                            nc.gpsimd.indirect_dma_start(
                                out=io["meta"], out_offset=bass.IndirectOffsetOnAxis(ap=pos[:, i:i + 1], axis=0),
                                in_=meta[:, i, :], in_offset=None).then_inc(s["meta_out"], 16)

            batches(pool, iteration)
            pool.wait_ge(s["meta_out"], 16 * QB * B)
            pool.wait_ge(s["wm_link"], 4 * B)
            nc.gpsimd.partition_all_reduce(sc[:, X_PA1:X_PA1 + 2], fam[:, 0:2], P, RMAX
                                           ).then_inc(s["allmax"], 1)
            pool.wait_ge(s["allmax"], 2)


def ffn_block(nc, io, sc, conf, esum):
    with ExitStack() as ctx:
        sb = lambda n, s, d: ctx.enter_context(nc.sbuf_tensor(n, s, d))
        sem = lambda n: ctx.enter_context(nc.semaphore(n))
        NP = 2 * HC
        HP, RING = 1024, 5
        wf = sb("wf", [P, E, NP, 2, 2048], F16)
        wstage = sb("wstage", [P, RING, HP], F32)
        mall = sb("mall", [P, TOK // P, MROW], F32)
        eslot = sb("eslot", [P, SLOTS], F32)
        eint = sb("eint", [P, SLOTS], I32)
        tint = sb("tint", [P, SLOTS], I32)
        n0 = sb("n0", [P, 1], F32)
        rec = sb("rec", [P, 4, MROW], F32)
        gidx = sb("gidx", [P, 4], I32)
        oidx = sb("oidx", [P, 2], I32)
        miss = sb("miss", [P, 1], F32)
        xg = sb("xg", [P, 4, D], F32)
        sg = sb("sg", [P, 2, D], F32)
        xn = sb("xn2", [P, D], F32)
        xT = sb("xT2", [P, 2, 2, D], F16)
        rl = sb("rl", [P, 2, 512], F32)
        a = sb("a", [P, 2, HC, 512], F32)
        aT = sb("aT", [P, 2, 2, 512], F16)
        z = sb("z", [P, D], F32)
        gt = sb("gt", [P, D], F32)
        ob = sb("ob", [P, D], F32)
        psF = [ctx.enter_context(nc.psum_tensor(f"psF{i}", [P, 512], F32)) for i in range(2)]
        psT = [ctx.enter_context(nc.psum_tensor(f"psU{i}", [P, 512], F32)) for i in range(2)]
        psX = ctx.enter_context(nc.psum_tensor("psX", [P, 512], F32))
        psY = [ctx.enter_context(nc.psum_tensor(f"psY{i}", [P, 512], F32)) for i in range(2)]
        names = ("m_in made ws_hi ws_lo e_table idx_ready ln_done X_done X_hi X_lo F_done f_relu f_sum "
                 "a_ready U_done U_hi U_lo Y_done z_ready g_exp g_ready o_ready ob_free apart_pool f_link out_done").split()
        s = {n: sem("f_" + n) for n in names}
        w_in = [sem(f"wf_in{i}") for i in range(RING)]
        x_got = [sem(f"x_got{i}") for i in range(4)]
        s_got = [sem(f"s_got{i}") for i in range(2)]
        block = ctx.enter_context(nc.Block())
        LOOPS = (SLOTS - 4) // 4

        def arrived(n, r, ring):
            return (n - (r % ring) + ring) * (16 // ring)

        def slots(eng, step):
            for n in range(-3, 1):
                step(n, n % 4)
            with eng.Fori(0, LOOPS) as it:
                for q in range(4):
                    step(it * 4 + (q + 1), (q + 1) % 4)
            for n in range(4 * LOOPS + 1, SLOTS + 1):
                step(n, n % 4)

        @block.sync
        def _(sp):
            for n in range(E * NP * 2):
                if n >= RING:
                    sp.wait_ge(s["ws_lo"], n - RING + 1)
                c = n % 2 * HP
                sp.dma_start(wstage[:, n % RING, :], io["wf"][n // 2, :, c:c + HP]).then_inc(w_in[n % RING], 16)
                if n == 0:
                    sp.dma_start(mall[:], io["meta"].rearrange("(t p) c -> p t c", p=P)).then_inc(s["m_in"], 16)

        @block.tensor
        def _(pe):
            def expert(eng_s):
                return pe.value_load(eint[0:1, bass.ds(eng_s, 1)], min_val=0, max_val=1)

            def w(e, piece, hl, c):
                return wf[:, bass.ds(e, 1), piece, hl, c * 512:(c + 1) * 512].rearrange("p o n -> p (o n)")

            def xtrans(n, r):
                wait(pe, s["ln_done"], n + 1)
                wait(pe, s["X_lo"], n)
                for kc in range(KC):
                    last = nc.tensor.transpose(psX[:, kc * P:(kc + 1) * P], xn[:, kc * P:(kc + 1) * P],
                                               conf[:, C_ID:C_ID + P])
                last.then_inc(s["X_done"], 1)

            def up(n, r, hc, e):
                t = n * HC + hc
                if hc == 0:
                    wait(pe, s["X_lo"], n + 1)
                if isinstance(n, int):
                    wait(pe, s["ws_lo"], 2 * (2 * hc + 1 + (NP if n > 0 else 0)))
                ps = psF[hc % 2]
                wait(pe, s["f_sum"], t - 1)
                k = 0
                for x, hl in ((0, 0), (1, 0), (0, 1)):
                    for kc in range(KC):
                        last = nc.tensor.matmul(ps[:], xT[:, r % 2, x, kc * P:(kc + 1) * P],
                                                w(e, 2 * hc, hl, kc), start=(k == 0), stop=(k == 3 * KC - 1))
                        k += 1
                last.then_inc(s["F_done"], 1)

            def turn(n, r, hc):
                t = n * HC + hc
                wait(pe, s["a_ready"], t + 1)
                wait(pe, s["U_lo"], t - 1)
                for q in range(4):
                    last = nc.tensor.transpose(psT[hc % 2][:, q * P:(q + 1) * P],
                                               a[:, r % 2, hc, q * P:(q + 1) * P], conf[:, C_ID:C_ID + P])
                last.then_inc(s["U_done"], 1)

            def down(n, r, hc, e):
                t = n * HC + hc
                if hc == 0:
                    wait(pe, s["z_ready"], n)
                if isinstance(n, int):
                    wait(pe, s["ws_lo"], 2 * (2 * hc + 2 + (NP if n > 0 else 0)))
                wait(pe, s["U_lo"], t + 1)
                k = 0
                for x, hl in ((0, 0), (1, 0), (0, 1)):
                    for q in range(4):
                        last = nc.tensor.matmul(psY[r % 2][:], aT[:, hc % 2, x, q * P:(q + 1) * P],
                                                w(e, 2 * hc + 1, hl, q), start=(hc == 0 and k == 0),
                                                stop=(hc == HC - 1 and k == 11))
                        k += 1
                last.then_inc(s["Y_done"], 1)

            def step(n, r):
                here, ahead = within(n, 0, SLOTS), within(n + 1, 0, SLOTS)
                e0 = expert(n) if here else None
                e1 = expert(n + 1) if ahead else None
                if ahead and not isinstance(n, int):
                    pe.wait_ge(s["ws_lo"], E * NP * 2)
                for hc in range(HC):
                    if here:
                        turn(n, r, hc)
                    if here and hc > 0:
                        down(n, r, hc - 1, e0)
                    if ahead:
                        up(n + 1, r + 1, hc, e1)
                    if hc == 1 and within(n + 2, 0, SLOTS):
                        xtrans(n + 2, r + 2)
                if here:
                    down(n, r, HC - 1, e0)

            pe.wait_ge(s["e_table"], 1)
            slots(pe, step)

        @block.scalar
        def _(act):
            act.wait_ge(s["made"], 1)

            def split(m):
                for n in range(m * 4, (m + 1) * 4 if m < E * HC else 0):
                    e, q, h = n // (2 * NP), n // 2 % NP, n % 2 * HP
                    act.wait_ge(w_in[n % RING], (n // RING + 1) * 16)
                    c = X_S1 + q % 2
                    nc.scalar.activation(wf[:, e, q, 0, h:h + HP], wstage[:, n % RING, :], ACT.Copy,
                                         scale=sc[:, c:c + 1]).then_inc(s["ws_hi"], 1)

            def relu(n, r, hc):
                t = n * HC + hc
                wait(act, s["F_done"], t + 1)
                wait(act, s["f_sum"], t - 1)
                nc.scalar.activation(rl[:, hc % 2, :], psF[hc % 2][:], ACT.Relu, scale=2.0 ** -28
                                     ).then_inc(s["f_relu"], 1)

            def uhi(n, r, hc):
                t = n * HC + hc
                wait(act, s["U_done"], t + 1)
                wait(act, s["Y_done"], t - 1)
                nc.scalar.activation(aT[:, hc % 2, 0, :], psT[hc % 2][:], ACT.Copy).then_inc(s["U_hi"], 1)

            def step(n, r):
                here, ahead = within(n, 0, SLOTS), within(n + 1, 0, SLOTS)
                if isinstance(n, int) and n == -1:
                    split(0)
                for hc in range(HC):
                    if here:
                        uhi(n, r, hc)
                    if isinstance(n, int) and n in (-1, 0):
                        split((n + 1) * HC + hc + 1)
                    if ahead:
                        relu(n + 1, r + 1, hc)
                    if hc == 1 and within(n - 1, 0, SLOTS):
                        wait(act, s["z_ready"], n + 1)
                        nc.scalar.activation(gt[:], gt[:], ACT.Exp, scale=-1.0).then_inc(s["g_exp"], 1)
                    if hc == 1 and within(n + 2, 0, SLOTS):
                        wait(act, s["X_done"], n + 3)
                        wait(act, s["F_done"], (n + 1) * HC)
                        nc.scalar.activation(xT[:, r % 2, 0, :], psX[:], ACT.Copy, scale=1024.0
                                             ).then_inc(s["X_hi"], 1)

            slots(act, step)

        @block.vector
        def _(dve):
            n_made = [0]

            def made(ins):
                n_made[0] += 1
                ins.then_inc(s["f_link"], 1)
                dve.wait_ge(s["f_link"], n_made[0])

            ts = nc.vector.tensor_scalar
            x = lambda c, n=1: sc[:, c:c + n]
            made(ts(x(X_PA1, 2), x(X_PA1, 2), 1e-9, None, ALU.max))
            made(ts(x(X_PA1, 2).bitcast(I32), x(X_PA1, 2).bitcast(I32), 0x7F800000, None, ALU.bitwise_and))
            made(nc.vector.reciprocal(x(X_S1, 2), x(X_PA1, 2)))
            made(ts(x(X_S1, 2), x(X_S1, 2), 2.0 ** 14, None, ALU.mult))
            made(nc.vector.tensor_tensor(x(X_CY), x(X_PA1), x(X_PA1), ALU.mult))
            made(nc.vector.tensor_tensor(x(X_CY), x(X_CY), x(X_PA2), ALU.mult))
            made(ts(x(X_CY), x(X_CY), 2.0 ** -8, None, ALU.mult))
            made(ts(n0[:], esum[:, 0:1], -1.0, float(TOK), ALU.mult, ALU.add))
            made(ts(n0[:], n0[:], float(TOK - 1), None, ALU.min))
            made(ts(eslot[:], conf[:, C_SLOT:C_SLOT + SLOTS], n0[:, 0:1], None, ALU.is_gt))
            made(nc.vector.tensor_copy(eint[:], eslot[:]))
            made(nc.vector.scalar_tensor_tensor(out=tint[:], in0=conf[:, C_SLOT:C_SLOT + SLOTS], scalar=1.0 / P,
                                                in1=eslot[:], op0=ALU.mult, op1=ALU.subtract))
            nc.vector.memset(miss[:], 0.0).then_inc(s["made"], 1)
            nc.vector.memset(z[:], 0.0).then_inc(s["e_table"], 1)
            nc.vector.memset(ob[:, 0:1], 0.0).then_inc(s["z_ready"], 1)
            dve.wait_ge(s["m_in"], 16)
            MADE = n_made[0]
            LK = 7

            def split(m):
                for n in range(m * 4, (m + 1) * 4 if m < E * HC else 0):
                    e, q, h = n // (2 * NP), n // 2 % NP, n % 2 * HP
                    dve.wait_ge(s["ws_hi"], n + 1)
                    c = X_S1 + q % 2
                    nc.vector.scalar_tensor_tensor(out=wf[:, e, q, 1, h:h + HP], in0=wstage[:, n % RING, :],
                                                   scalar=sc[:, c:c + 1], in1=wf[:, e, q, 0, h:h + HP],
                                                   op0=ALU.mult, op1=ALU.subtract).then_inc(s["ws_lo"], 1)

            def fetch(n, r):
                tile = dve.value_load(tint[0:1, bass.ds(n, 1)], min_val=0, max_val=TOK // P - 1)
                src = mall[:, bass.ds(tile, 1), :].rearrange("p o c -> p (o c)")
                nc.vector.tensor_copy(rec[:, r % 4, :], src)
                nc.vector.tensor_copy(gidx[:, r % 4:r % 4 + 1], src[:, 0:1]).then_inc(s["idx_ready"], 1)

            def total(n, r, hc):
                t = n * HC + hc
                wait(dve, s["f_relu"], t + 1)
                wait(dve, s["U_done"], t - 2 * HC + 1)
                nc.vector.scalar_tensor_tensor(out=a[:, r % 2, hc, :], in0=psF[hc % 2][:], scalar=2.0 ** -28,
                                               in1=rl[:, hc % 2, :], op0=ALU.mult, op1=ALU.add
                                               ).then_inc(s["f_sum"], 1)

            def ulo(n, r, hc):
                t = n * HC + hc
                wait(dve, s["U_hi"], t + 1)
                nc.vector.tensor_tensor(aT[:, hc % 2, 1, :], psT[hc % 2][:], aT[:, hc % 2, 0, :], ALU.subtract
                                        ).then_inc(s["U_lo"], 1)

            def step(n, r):
                here, ahead = within(n, 0, SLOTS), within(n + 1, 0, SLOTS)
                done = within(n - 1, 0, SLOTS)
                k = [0]

                def link(ins):
                    k[0] += 1
                    ins.then_inc(s["f_link"], 1)
                    dve.wait_ge(s["f_link"], (n - 1) * LK + k[0] + MADE)

                if done:
                    m = n - 1
                    rm = (r - 1) % 4
                    wait(dve, s["Y_done"], n * HC)
                    link(ts(z[:], psY[rm % 2][:], rec[:, rm, 1:2], x(X_CY), ALU.mult, ALU.mult))
                    nc.vector.tensor_scalar(gt[:], z[:], -80.0, None, ALU.max).then_inc(s["z_ready"], 1)
                if isinstance(n, int) and n == -1:
                    split(0)
                for hc in range(HC):
                    if here:
                        ulo(n, r, hc)
                    if isinstance(n, int) and n in (-1, 0):
                        split((n + 1) * HC + hc + 1)
                    if ahead:
                        total(n + 1, r + 1, hc)
                    if done and hc == 1:
                        wait(dve, s["g_exp"], n)
                        link(ts(gt[:], gt[:], 1.0, None, ALU.add))
                        link(nc.vector.reciprocal(gt[:], gt[:]))
                    if done and hc == 2:
                        wait(dve, s_got[rm % 2], arrived(n - 1, rm, 2))
                        wait(dve, s["ob_free"], n)
                        link(nc.vector.tensor_tensor(z[:], z[:], gt[:], ALU.mult))
                        link(nc.vector.tensor_tensor(z[:], z[:], sg[:, rm % 2, :], ALU.mult))
                        link(ts(miss[:], rec[:, rm, 2:3], esl(n - 1), float(OOB), ALU.not_equal, ALU.mult))
                        link(nc.vector.tensor_tensor(oidx[:, rm % 2:rm % 2 + 1], miss[:], rec[:, rm, 0:1],
                                                     ALU.add))
                        nc.vector.tensor_tensor(ob[:], z[:], xg[:, rm, :], ALU.add).then_inc(s["o_ready"], 1)
                        dve.wait_ge(s["o_ready"], n)
                    if hc == 2 and within(n + 3, 0, SLOTS):
                        fetch(n + 3, r + 3)
                    if hc == 0 and within(n + 2, 0, SLOTS):
                        r2 = (r + 2) % 4
                        wait(dve, x_got[r2], arrived(n + 2, r2, 4))
                        wait(dve, s["X_done"], n + 2)
                        dve.wait_ge(s["idx_ready"], n + 3)
                        nc.vector.tensor_scalar(xn[:], xg[:, r2, :], rec[:, r2, 3:4], rec[:, r2, 4:5],
                                                ALU.subtract, ALU.mult).then_inc(s["ln_done"], 1)
                    if hc == 1 and within(n + 2, 0, SLOTS):
                        wait(dve, s["X_hi"], n + 3)
                        nc.vector.scalar_tensor_tensor(out=xT[:, r % 2, 1, :], in0=psX[:], scalar=1024.0,
                                                       in1=xT[:, r % 2, 0, :], op0=ALU.mult, op1=ALU.subtract
                                                       ).then_inc(s["X_lo"], 1)
                assert not done or k[0] == LK

            def esl(n):
                return eslot[:, bass.ds(n, 1)]

            slots(dve, step)

        @block.gpsimd
        def _(pool):
            def gather(dst, src, r, sm):
                nc.gpsimd.indirect_dma_start(out=dst, out_offset=None, in_=src,
                                             in_offset=bass.IndirectOffsetOnAxis(ap=gidx[:, r % 4:r % 4 + 1], axis=0)
                                             ).then_inc(sm, 16)

            def step(n, r):
                done = within(n - 1, 0, SLOTS)
                for hc in range(HC):
                    if within(n + 1, 0, SLOTS):
                        t = (n + 1) * HC + hc
                        wait(pool, s["f_sum"], t + 1, s["apart_pool"])
                        at = a[:, (r + 1) % 2, hc, :]
                        nc.gpsimd.tensor_tensor(at, at, at, ALU.mult).then_inc(s["a_ready"], 1)
                    if hc == 2 and done:
                        wait(pool, s["o_ready"], n, s["apart_pool"])
                        rm = (r - 1) % 4
                        nc.gpsimd.indirect_dma_start(
                            out=io["out"],
                            out_offset=bass.IndirectOffsetOnAxis(ap=oidx[:, rm % 2:rm % 2 + 1], axis=0),
                            in_=ob[:], in_offset=None, bounds_check=TOK - 1, oob_is_err=False
                        ).then_inc(s["out_done"], 16)
                    if hc == 2 and within(n + 3, 0, SLOTS):
                        wait(pool, s["idx_ready"], n + 4, s["apart_pool"])
                        gather(xg[:, (r + 3) % 4, :], io["x"], r + 3, x_got[(r + 3) % 4])
                    if hc == 2 and within(n + 1, 0, SLOTS):
                        gather(sg[:, (r + 1) % 2, :], io["s"], r + 1, s_got[(r + 1) % 2])
                if done:
                    wait(pool, s["out_done"], n * 16, s["apart_pool"])
                    pool.sem_inc(s["ob_free"], 1)

            pool.sem_inc(s["ob_free"], 1)
            slots(pool, step)
            pool.wait_ge(s["out_done"], SLOTS * 16)


def build(nc, x, wqkv, bqkv, wout, bout, wr, wf, const, out):
    io = {"x": x, "wqkv": wqkv, "bqkv": bqkv, "wout": wout, "bout": bout, "wr": wr, "wf": wf,
          "const": const, "out": out,
          "s": nc.dram_tensor("attn_out", [TOK, D], F32).ap(),
          "meta": nc.dram_tensor("route", [TOK, MROW], F32).ap(),
          "qk": nc.dram_tensor("qk_parts", [2, 2, 2, P, S], F16).ap()}
    with ExitStack() as ctx:
        sc = ctx.enter_context(nc.sbuf_tensor("sc", [P, X_N], F32))
        conf = ctx.enter_context(nc.sbuf_tensor("conf", [P, C_N], F32))
        esum = ctx.enter_context(nc.sbuf_tensor("esum", [P, 1], F32))
        attention_block(nc, io, sc, conf, esum)
        ffn_block(nc, io, sc, conf, esum)


def kernel(L0_attn_x, L0_attn_Wqkv, L0_attn_b_qkv, L0_attn_Wout, L0_attn_b_out,
           L0_ffn_w_router, L0_ffn_w_fc, L0_ffn_w_proj):
    import concourse.bacc as bacc
    from concourse.bass_utils import run_bass_kernel_spmd

    def lhs(w, k):
        w = np.asarray(w)
        return np.ascontiguousarray(w.T.reshape(k, P, -1).transpose(1, 0, 2).reshape(P, -1))

    w1 = np.asarray(L0_ffn_w_fc).reshape(E, HC, 512, KC, P).transpose(0, 1, 4, 3, 2).reshape(E, HC, P, 2048)
    w2 = np.asarray(L0_ffn_w_proj).reshape(E, D, HC, 4, P).transpose(0, 2, 4, 3, 1).reshape(E, HC, P, 2048)
    arrays = {
        "x": np.ascontiguousarray(np.asarray(L0_attn_x).reshape(TOK, D)),
        "wqkv": lhs(L0_attn_Wqkv, KC),
        "bqkv": np.ascontiguousarray(np.asarray(L0_attn_b_qkv).reshape(3 * NG, P).T),
        "wout": lhs(L0_attn_Wout, NG),
        "bout": np.ascontiguousarray(np.broadcast_to(np.asarray(L0_attn_b_out), (P, D))),
        "wr": lhs(L0_ffn_w_router, KC),
        "wf": np.ascontiguousarray(np.stack([w1, w2], 2).reshape(E * HC * 2, P, 2048)),
        "const": constants(),
    }
    nc = bacc.Bacc("TRN2", target_bir_lowering=False, num_devices=1)
    args = [nc.dram_tensor("in_" + n, a.shape, mybir.dt.from_np(a.dtype), kind="ExternalInput").ap()
            for n, a in arrays.items()]
    args.append(nc.dram_tensor("out_x", (TOK, D), F32, kind="ExternalOutput").ap())
    build(nc, *args)
    r = run_bass_kernel_spmd(nc, [{"in_" + n: a for n, a in arrays.items()}], core_ids=[0])
    return r.results[0]["out_x"].reshape(B, S, D)
```

```python
import concourse.bass as bass
from concourse import mybir
from concourse.alu_op_type import AluOpType as ALU
from contextlib import ExitStack
import numpy as np

P = 128
B, S, D = 8, 512, 512
H, HD = 16, 32
TOK = B * S
KC = D // P
QB = S // P
HG = P // HD
NG = H // HG
NU = B * NG
E, HID = 2, 2048
HC = HID // 512
SLOTS = TOK // P + 1
MROW = 8
MASK = -float(2 ** 40)
OOB = 8192

ROWOFF = [P * i * (i + 1) // 2 for i in range(QB)]
CAUSAL = P * QB * (QB + 1) // 2
SEG = {0: 0, 1: 512, 3: 896, 2: 1024}
TJOBS = [[0], [1, 3], [2]]

F32, F16, I32 = mybir.dt.float32, mybir.dt.float16, mybir.dt.int32
ACT = mybir.ActivationFunctionType
AX = mybir.AxisListType
RMAX = bass.bass_isa.ReduceOp.max

C_ID, C_LT, C_BASE, C_F, C_TOK, C_NSL, C_SLOT = 0, 128, 256, 768, 772, 776, 792
C_N = C_SLOT + SLOTS
(X_SWQ, X_RPM, X_SWO, X_SWR, X_PA, X_PM, X_PAO, X_PAR, X_CK, X_CC, X_CS, X_CR, X_T0, X_T1,
 X_S1, X_S2, X_CY, X_PA1, X_PA2, X_N) = range(20)


def constants():
    c = np.zeros((P, C_N), np.float32)
    p = np.arange(P)
    c[:, C_ID:C_ID + P] = np.eye(P)
    c[:, C_LT:C_LT + P] = p[:, None] < p[None, :]
    k = np.arange(S)
    c[:, C_BASE:C_BASE + S] = k[None, :] - (S - 1)
    c[:, C_BASE + S - P:C_BASE + S] += np.where(p[None, :] > p[:, None], MASK, 0.0)
    slope = 2.0 ** (-(np.arange(H) + 1) * 8.0 / H)
    for g in range(NG):
        c[:, C_F + g] = (HD ** -0.5) / slope[g * HG + p // HD]
    for i in range(QB):
        c[:, C_TOK + i] = i * P + p
    c[:, C_NSL:C_NSL + H] = -slope[None, :]
    c[:, C_SLOT:C_SLOT + SLOTS] = P * np.arange(SLOTS)[None, :]
    return c


def wait(eng, sem, value, apart=None):
    if isinstance(value, int) and value <= 0:
        return
    eng.wait_ge(sem, value)
    if apart is not None and not isinstance(value, int):
        eng.sem_inc(apart, 1)


def within(n, lo, hi):
    return not isinstance(n, int) or lo <= n < hi


def batches(eng, iteration):
    iteration(-1, 1)
    iteration(0, 0)
    with eng.Fori(0, (B - 2) // 2) as it:
        iteration(it * 2 + 1, 1)
        iteration(it * 2 + 2, 0)
    iteration(B - 1, 1)
    iteration(B, 0)


WEIGHTS = ["q", "k", "logits", "v", "o"]
JOBS = [("q", 0, 2), ("ctx", -1, 3), ("k", 0, 2), ("q", 0, 3), ("k", 0, 3),
        ("o", -1, 0), ("x", 1, 0), ("ctx", 0, 0), ("o", -1, 1), ("x", 1, 1),
        ("x", 1, 2), ("o", -1, 2), ("o", -1, 3), ("x", 1, 3),
        ("q", 1, 0), ("ctx", 0, 1), ("k", 1, 0), ("logits", 1, 0), ("v", 1, 0),
        ("v", 1, 1), ("q", 1, 1), ("ctx", 0, 2), ("k", 1, 1), ("rank", 1, 0),
        ("v", 1, 2), ("v", 1, 3)]
STEP = [(0, 1), (2,), (3,), (4,), (5, 6, 7), (8, 9), (10, 11), (12, 13),
        (14, 15), (16,), (17, 18), (19,), (20, 21), (22, 23), (24,), (25,)]
WMAX_AT = (5, 8, 12, 14)
NJOB = len(JOBS)
ABANKS = 2
S_LEAD, M_LEAD, E_LEAD, N_LEAD = 4, 3, 2, 1


def job_exists(b, pos):
    return not isinstance(b, int) or 0 <= b + JOBS[pos][1] < B


def head_at(b, n):
    return (b, n) if 0 <= n < H else ((b + 1, n - H) if n >= H else (b - 1, n + H))


def attention_block(nc, io, sc, conf, esum, mall, eslot, eint, tint):
    with ExitStack() as ctx:
        sb = lambda n, s, d: ctx.enter_context(nc.sbuf_tensor(n, s, d))
        sem = lambda n: ctx.enter_context(nc.semaphore(n))
        wqkv = sb("wqkv", [P, KC, 2, 3 * D], F16)
        wout = sb("wout", [P, NG, 2, D], F16)
        wr = sb("wr", [P, KC, 2, E], F16)
        wr_f = sb("wr_f", [P, KC * E], F32)
        bqk = sb("bqk", [P, 3 * NG], F32)
        bqs = sb("bqs", [P, 3 * NG], F32)
        cq = sb("cq", [P, NG], F32)
        nsl = sb("nsl", [P, H], F32)
        base = sb("base", [P, S], F32)
        bout = sb("bout", [P, D], F32)
        lt16 = sb("lt16", [P, P], F16)
        ones16 = sb("ones16", [P, P], F16)
        tid = sb("tid", [P, QB], F32)
        am = sb("am", [P, 8], F32)
        n0 = sb("n0", [P, 1], F32)
        amr = sb("amr", [P, 8], F32)
        fam = sb("fam", [P, 4], F32)
        xin = sb("xin", [P, QB, D], F32)
        xn = sb("xn", [P, QB, D], F32)
        stat = sb("stat", [P, QB, 6], F32)
        mv = sb("mv", [P, QB, 2], F32)
        veps = sb("veps", [P, QB], F32)
        half = sb("half", [P, QB], F32)
        rstd = sb("rstd", [P, 2, QB], F32)
        xT = sb("xT", [P, 2, 2, KC, S], F16)
        stage = sb("stage", [P, 2, S], F32)
        pre = sb("pre", [P, 2, 2, S], F16)
        qs = sb("qs", [P, 2, HG, S], F16)
        ks = sb("ks", [P, 2, HG, S], F16)
        v = sb("v", [P, 2, 2, QB, D], F16)
        pr = sb("pr", [P, HG, CAUSAL], F32)
        mn = sb("mn", [P, HG * QB], F32)
        den = sb("den", [P, HG * QB], F32)
        rden = sb("rden", [P, HG * QB], F32)
        pt = sb("pt", [P, 2, 2, HG, CAUSAL], F16)
        cf = sb("cf", [P, S], F32)
        cx = sb("cx", [P, NG, 2, S], F16)
        so = sb("so", [P, QB, D], F32)
        wst = sb("wst", [P, 2048], F32)
        lg = sb("lg", [P, QB, E], F32)
        dl = sb("dl", [P, QB], F32)
        nd = sb("nd", [P, QB], F32)
        ex = sb("ex", [P, QB], F32)
        e16 = sb("e16", [P, QB + 1], F16)
        epre = sb("epre", [P, QB + 1], F16)
        ef = sb("ef", [P, QB + 1], F32)
        rk = sb("rk", [P, QB + 1], F32)
        t0 = sb("t0", [P, QB], F32)
        t1 = sb("t1", [P, QB], F32)
        pos = sb("pos", [P, QB], I32)
        meta = sb("meta", [P, QB, MROW], F32)

        psA = [ctx.enter_context(nc.psum_tensor(f"psA{i}", [P, 512], F32)) for i in range(ABANKS)]
        psS = [ctx.enter_context(nc.psum_tensor(f"psS{i}", [P, 512], F32)) for i in range(3)]
        rows = [psS[0][:, 0:P], psS[0][:, P:3 * P], psS[1][:, 0:3 * P], psS[2][:, 0:4 * P]]
        psT = [ctx.enter_context(nc.psum_tensor(f"psT{i}", [P, 512], F32)) for i in range(3)]

        names = ("const_in w_in wr_in bout_in largest absmax allmax scales biases w_split_hi w_split_lo setup "
                 "ln_stats rstd_ready xn_ready xT_done xT_hi xT_lo V_done V_hi V_lo "
                 "qk_done qk_staged qk_hi qk_lo S_done ttr_done exp_done rden_done norm_done "
                 "T_done T_hi T_lo PV_done ctx_staged ctx_hi ctx_lo O_done O_evac "
                 "R_done R_part R2_done logits_read rank_read e_ready nd_ready rexp_done meta_ready m_in wmax_in wmax_done "
                 "apart_dve apart_sp apart_pool dve_link wm_link pool_link meta_out").split()
        s = {n: sem(n) for n in names}
        x_in = [sem(f"x_in{i}") for i in range(QB)]
        s_out = [sem(f"s_out{i}") for i in range(QB)]
        wq_in = [sem(f"wq_in{i}") for i in range(KC)]
        stored = [sem("q_stored"), sem("k_stored")]
        stacked = [[sem(f"{n}_stacked{p}") for p in range(2)] for n in "qk"]

        wflat = pt[:, :, :, :, :].rearrange("p a b h n -> p (a b h n)").bitcast(F32)
        wq_f = wflat[:, 0:KC * 3 * D]
        wo_f = wflat[:, KC * 3 * D:KC * 3 * D + NG * D]

        def weight_parts():
            for i in range(3):
                if i == 2:
                    yield wr[:, :, 0, :], wr[:, :, 1, :], wr_f[:].rearrange("p (k n) -> p k n", n=E), X_SWR
                c = slice(i * D, (i + 1) * D)
                yield (wqkv[:, :, 0, c], wqkv[:, :, 1, c],
                       wq_f.rearrange("p (k n) -> p k n", n=3 * D)[:, :, c], X_SWQ)
            yield wout[:, :, 0, :], wout[:, :, 1, :], wo_f.rearrange("p (k n) -> p k n", n=D), X_SWO

        def job_count(b, p):
            kind, db, i = JOBS[p]
            if kind in ("logits", "rank"):
                return s[kind + "_read"], b + db + 1
            n = (b + db) * QB + i
            if kind == "ctx":
                return s["ctx_staged"], n + 1
            if kind in ("q", "k"):
                return s["qk_staged"], n * 2 + 1 + (kind == "k")
            return s[{"o": "O_evac", "x": "xT_lo", "v": "V_lo"}[kind]], n + 1

        def jobs(b, odd, step, kinds=("q", "k", "v", "x", "o", "logits", "rank")):
            for p in STEP[step]:
                kind, db, i = JOBS[p]
                if job_exists(b, p) and kind in kinds:
                    yield kind, b + db, i, (odd + db) % 2, psA[p % ABANKS]

        block = ctx.enter_context(nc.Block())

        @block.sync
        def _(sp):
            for i in range(QB):
                sp.sem_inc(s_out[i], 16)
            for i in range(QB):
                sp.dma_start(xin[:, i, :], io["x"][i * P:(i + 1) * P, :]).then_inc(x_in[i], 16)
                if i == 1:
                    sp.dma_start(conf[:], io["const"]).then_inc(s["const_in"], 16)
            sp.dma_start(wr_f[:], io["wr"]).then_inc(s["wr_in"], 16)
            sp.dma_start(bqk[:], io["bqkv"]).then_inc(s["wr_in"], 16)
            sp.dma_start(wo_f, io["wout"]).then_inc(s["w_in"], 16)
            for kc in range(KC):
                c = kc * 3 * D
                sp.dma_start(wq_f[:, c:c + 3 * D], io["wqkv"][:, c:c + 3 * D]).then_inc(wq_in[kc], 16)
            sp.dma_start(bout[:], io["bout"]).then_inc(s["bout_in"], 16)

            def stack(b, g):
                u = b * NG + g
                if not within(u, 0, NU):
                    return
                par = g % 2
                for w, dst, parts in ((0, qs, (0, 1, 0, 1)), (1, ks, (0, 0, 1, 1))):
                    wait(sp, s["qk_hi"], u * 2 + 1 + w, s["apart_sp"])
                    wait(sp, s["qk_lo"], u * 2 + 1 + w, s["apart_sp"])
                    wait(sp, stacked[w][par], (b * 2 + g // 2) * 64, s["apart_sp"])
                    sp.dma_start(io["qk"][w, par].rearrange("a p n -> p a n"),
                                 pre[:, w, :, :]).then_inc(stored[w], 16)
                    wait(sp, stored[w], (u + 1) * 16, s["apart_sp"])
                    wait(sp, s["S_done"], (u - 1) * 16, s["apart_sp"])
                    for r in range(4):
                        sp.dma_start(dst[r * HD:(r + 1) * HD, par, :, :],
                                     io["qk"][w, par, parts[r]].rearrange("(j d) n -> d j n", j=HG)
                                     ).then_inc(stacked[w][par], 16)

            def iteration(b, odd):
                if within(b, 0, B - 1):
                    for i in range(QB):
                        wait(sp, s["xn_ready"], b * QB + i + 1, s["apart_sp"])
                        sp.dma_start(xin[:, i, :], io["x"][bass.ds((b + 1) * S + i * P, P), :]
                                     ).then_inc(x_in[i], 16)
                if within(b, 0, B):
                    wait(sp, s["wmax_done"], b * 4, s["apart_sp"])
                    sp.dma_start(wst[:], io["wf"][bass.ds(b * 2, 1)].rearrange("o p n -> (o p) n")
                                 ).then_inc(s["wmax_in"], 16)
                    stack(b, 2)
                if within(b, 0, B):
                    stack(b, 3)
                if within(b, 1, B + 1):
                    for i in range(QB):
                        wait(sp, s["O_evac"], (b - 1) * QB + i + 1, s["apart_sp"])
                        sp.dma_start(io["s"][bass.ds((b - 1) * S + i * P, P), :], so[:, i, :]
                                     ).then_inc(s_out[i], 16)
                if within(b, 0, B):
                    wait(sp, s["wmax_done"], b * 4 + 2, s["apart_sp"])
                    sp.dma_start(wst[:], io["wf"][bass.ds(b * 2 + 1, 1)].rearrange("o p n -> (o p) n")
                                 ).then_inc(s["wmax_in"], 16)
                if within(b, -1, B - 1):
                    stack(b + 1, 0)
                    stack(b + 1, 1)

            batches(sp, iteration)
            sp.wait_ge(s["meta_out"], 16 * QB * B)
            sp.dma_start(mall[:], io["meta"].rearrange("(t p) c -> p t c", p=P)).then_inc(s["m_in"], 16)
            sp.wait_ge(s["m_in"], 16)
            for i in range(QB):
                sp.wait_ge(s_out[i], 16 * (B + 1))

        @block.tensor
        def _(pe):
            def bank(b, p):
                bb, q = b, p - ABANKS
                while True:
                    if q < 0:
                        bb, q = bb - 1, q + NJOB
                    if isinstance(bb, int) and bb < -1:
                        break
                    if job_exists(bb, q):
                        if JOBS[p] != ("q", 1, 0) or JOBS[q][0] != "x":
                            wait(pe, *job_count(bb, q))
                        break
                    q -= ABANKS
                return psA[p % ABANKS]

            def products(ps, pairs, mid, done):
                for n, (a, x) in enumerate(pairs):
                    if n == len(pairs) // 2:
                        mid()
                    last = nc.tensor.matmul(ps, a, x, start=(n == 0), stop=(n == len(pairs) - 1))
                last.then_inc(done, 1)

            PARTS = ((0, 0), (1, 0), (0, 1))

            def job(b, odd, p, mid):
                kind, db, i = JOBS[p]
                batch, par = b + db, (odd + db) % 2
                if isinstance(b, int) and b == -1 and kind in WEIGHTS:
                    pe.wait_ge(s["w_split_lo"], WEIGHTS.index(kind) + 1)
                if isinstance(b, int) and b == 0 and (kind, i) == ("o", 0):
                    pe.wait_ge(s["w_split_lo"], len(WEIGHTS))
                if kind in ("q", "k"):
                    if (kind, db, i) == ("q", 1, 0):
                        wait(pe, s["xT_lo"], (batch + 1) * QB)
                    ps = bank(b, p)
                    col = (kind == "k") * D + i * P
                    products(ps[:], [(wqkv[:, kc, a, col:col + P], xT[:, par, x, kc, :])
                                     for x, a in PARTS for kc in range(KC)], mid, s["qk_done"])
                elif kind == "v":
                    ps = bank(b, p)
                    products(ps[:], [(xT[:, par, x, kc, i * P:(i + 1) * P], wqkv[:, kc, a, 2 * D:3 * D])
                                     for x, a in PARTS for kc in range(KC)], mid, s["V_done"])
                elif kind == "o":
                    ps = bank(b, p)
                    if i == 0:
                        wait(pe, s["ctx_hi"], (batch + 1) * NG)
                        wait(pe, s["ctx_lo"], (batch + 1) * NG)
                    products(ps[:], [(cx[:, g, x, i * P:(i + 1) * P], wout[:, g, a, :])
                                     for x, a in PARTS for g in range(NG)], mid, s["O_done"])
                elif kind == "logits":
                    ps = bank(b, p)
                    for t in range(QB):
                        products(ps[:, t * E:(t + 1) * E],
                                 [(xT[:, par, x, kc, t * P:(t + 1) * P], wr[:, kc, a, :])
                                  for x, a in PARTS for kc in range(KC)],
                                 mid if t == QB - 1 else lambda: None,
                                 s["R_done"] if t == QB - 1 else s["R_part"])
                elif kind == "rank":
                    ps = bank(b, p)
                    wait(pe, s["e_ready"], batch + 1)
                    nc.tensor.matmul(ps[:, 0:QB + 1], lt16[:], e16[:], start=True, stop=False)
                    nc.tensor.matmul(ps[:, 0:QB + 1], ones16[:], epre[:], start=False, stop=True
                                     ).then_inc(s["R2_done"], 1)
                else:
                    ps = bank(b, p)
                    mid()
                    wait(pe, s["xn_ready"], batch * QB + i + 1)
                    for kc in range(KC):
                        last = nc.tensor.transpose(ps[:, kc * P:(kc + 1) * P], xn[:, i, kc * P:(kc + 1) * P],
                                                   conf[:, C_ID:C_ID + P])
                    last.then_inc(s["xT_done"], 1)

            def scores(b, h):
                g, j = h // HG, h % HG
                par = g % 2
                n = (b * H + h) * QB
                if j == 0:
                    for w in range(2):
                        wait(pe, stacked[w][par], (b * 2 + g // 2 + 1) * 64)
                for i in range(QB):
                    if i != 1:
                        wait(pe, s["ttr_done"], n - QB + max(i, 1) + 1)
                    nc.tensor.matmul(rows[i], qs[:, par, j, i * P:(i + 1) * P],
                                     ks[:, par, j, 0:(i + 1) * P], start=True, stop=True
                                     ).then_inc(s["S_done"], 1)

            def ptrans(b, g, j, r):
                if not within(b, 0, B):
                    return
                h = b * H + g * HG + j
                if r == 0:
                    wait(pe, s["norm_done"], (h + 1) * QB)
                ps = psT[r]
                wait(pe, s["T_lo"], h * 3 + r - 2)
                kbs = TJOBS[r]
                for kb in kbs:
                    for i in range(kb, QB):
                        o = SEG[kb] - SEG[kbs[0]] + (i - kb) * P
                        c = ROWOFF[i] + kb * P
                        last = nc.tensor.transpose(ps[:, o:o + P], pr[:, j, c:c + P],
                                                   conf[:, C_ID:C_ID + P])
                last.then_inc(s["T_done"], 1)

            def pv(b, g, par, psC):
                u = b * NG + g
                wait(pe, s["T_lo"], (u + 1) * 12)
                if g == 0:
                    wait(pe, s["V_lo"], (b + 1) * QB)
                for kb in range(QB):
                    w = S - kb * P
                    for n, (x, a) in enumerate(((0, 0), (0, 1), (1, 0))):
                        for j in range(HG):
                            c = (g * HG + j) * HD
                            last = nc.tensor.matmul(
                                psC[j * HD:(j + 1) * HD, kb * P:S], v[:, par, a, kb, c:c + HD],
                                pt[:, g % 2, x, j, SEG[kb]:SEG[kb] + w],
                                start=(kb == 0 and n == 0), stop=(kb == QB - 1 and n == 2))
                last.then_inc(s["PV_done"], 1)

            def iteration(b, odd):
                for step in range(H):
                    g, j = step // HG, step % HG
                    ptrans(b, g, j, 0)
                    todo = [p for p in STEP[step] if job_exists(b, p) and JOBS[p][0] != "ctx"]

                    def between():
                        ptrans(b, g, j, 1)

                    if not todo:
                        between()
                    for n, p in enumerate(todo):
                        job(b, odd, p, between if n == 0 else lambda: None)
                    ptrans(b, g, j, 2)
                    hb, h = head_at(b, step + S_LEAD)
                    if within(hb, 0, B):
                        scores(hb, h)
                    for p in STEP[step]:
                        if JOBS[p][0] == "ctx" and job_exists(b, p):
                            db = JOBS[p][1]
                            pv(b + db, JOBS[p][2], (odd + db) % 2, bank(b, p))

            pe.sem_inc(s["O_done"], 1)
            pe.wait_ge(s["const_in"], 16)
            batches(pe, iteration)

        @block.scalar
        def _(act):
            def prepare():
                act.wait_ge(s["scales"], 1)
                for hi, _, src, c in weight_parts():
                    nc.scalar.activation(hi, src, ACT.Copy, scale=sc[:, c:c + 1]).then_inc(s["w_split_hi"], 1)
                act.wait_ge(s["biases"], 1)

            def read_out(kind, b, i, par, ps):
                if kind in ("q", "k"):
                    w, n = int(kind == "k"), (b * NG + i) * 2
                    wait(act, s["qk_done"], n + 1 + w)
                    wait(act, s["qk_lo"], n - 1 + w)
                    nc.scalar.activation(stage[:, w, :], ps[:], ACT.Identity,
                                         bias=bqs[:, w * NG + i:w * NG + i + 1],
                                         scale=cq[:, i:i + 1] if w == 0 else sc[:, X_CK:X_CK + 1]
                                         ).then_inc(s["qk_staged"], 1)
                elif kind == "ctx":
                    u = b * NG + i
                    wait(act, s["PV_done"], u + 1)
                    wait(act, s["ctx_lo"], u)
                    nc.scalar.activation(cf[:], ps[:], ACT.Identity, bias=bqs[:, 2 * NG + i:2 * NG + i + 1],
                                         scale=sc[:, X_CC:X_CC + 1]).then_inc(s["ctx_staged"], 1)
                elif kind == "x":
                    if i == 0:
                        wait(act, s["V_done"], (b - 1) * QB)
                        wait(act, s["qk_done"], (b - 1) * 2 * NG)
                        wait(act, s["R_done"], b - 1)
                    wait(act, s["xT_done"], b * QB + i + 1)
                    nc.scalar.activation(xT[:, par, 0, :, i * P:(i + 1) * P],
                                         ps[:].rearrange("p (k n) -> p k n", k=KC),
                                         ACT.Copy, scale=1024.0).then_inc(s["xT_hi"], 1)
                elif kind == "v":
                    wait(act, s["V_done"], b * QB + i + 1)
                    if i == 0:
                        wait(act, s["PV_done"], (b - 1) * NG)
                    nc.scalar.activation(v[:, par, 0, i, :], ps[:], ACT.Copy,
                                         scale=2.0 ** -19).then_inc(s["V_hi"], 1)

            def iteration(b, odd):
                more = within(b, -1, B - 1)
                for step in range(H):
                    g, j = step // HG, step % HG
                    if isinstance(b, int) and b == -1 and step == 8:
                        prepare()
                    hd = b * H + step
                    hb, h = head_at(b, step + E_LEAD)

                    def high(r):
                        if not within(b, 0, B):
                            return
                        kbs = TJOBS[r]
                        w = sum(S - kb * P for kb in kbs)
                        o = SEG[kbs[0]]
                        if r == 0 and j == 0:
                            wait(act, s["PV_done"], b * NG + g - 1)
                        wait(act, s["T_done"], hd * 3 + r + 1)
                        nc.scalar.activation(pt[:, g % 2, 0, j, o:o + w],
                                             psT[r][:, 0:w], ACT.Copy
                                             ).then_inc(s["T_hi"], 1)

                    def exps(i):
                        if not within(hb, 0, B):
                            return
                        c = (h % HG) * QB + i
                        if i == 0:
                            wait(act, s["rden_done"], hb * H + h - HG + 1)
                        wait(act, s["ttr_done"], (hb * H + h) * QB + i + 1)
                        p_ = pr[:, h % HG, ROWOFF[i]:ROWOFF[i] + (i + 1) * P]
                        nc.scalar.activation(p_, p_, ACT.Exp, bias=mn[:, c:c + 1], scale=-1.0,
                                             accum_out=den[:, c:c + 1]).then_inc(s["exp_done"], 1)

                    if j == 1:
                        for args in jobs(b, odd, step - 1, ("ctx",)):
                            read_out(*args)
                    high(0)
                    exps(0)
                    exps(1)
                    high(1)
                    exps(2)
                    for args in jobs(b, odd, step):
                        read_out(*args)
                    high(2)
                    exps(3)
                    if more and step == 12:
                        wait(act, s["nd_ready"], b + 2)
                        nc.scalar.activation(ex[:], nd[:], ACT.Exp).then_inc(s["rexp_done"], 1)

            batches(act, iteration)

        @block.vector
        def _(dve):
            n_setup = [0]

            def setup(ins):
                n_setup[0] += 1
                ins.then_inc(s["setup"], 1)
                dve.wait_ge(s["setup"], n_setup[0])

            nc.vector.memset(half[:], -0.5)
            nc.vector.memset(esum[:], 0.0)
            nc.vector.memset(fam[:], 0.0)
            nc.vector.memset(ones16[:], 1.0)
            nc.vector.memset(e16[:], 0.0)
            nc.vector.memset(epre[:], 0.0)
            nc.vector.memset(am[:], 0.0)
            nc.vector.memset(meta[:], 0.0)
            setup(nc.vector.memset(t0[:], 0.0))
            x = lambda c, n=1: sc[:, c:c + n]
            ts = nc.vector.tensor_scalar

            def pow2(dst, src):
                setup(ts(dst.bitcast(I32), src.bitcast(I32), 0x7F800000, None, ALU.bitwise_and))

            def magnitudes(step):
                def largest(c, src, *arrived):
                    for sm, value in arrived:
                        dve.wait_ge(sm, value)
                    nc.vector.tensor_reduce(am[:, c:c + 1], src, AX.X, ALU.max, apply_absolute_value=True)

                if step == 4:
                    largest(1, bqk[:, :], (s["wr_in"], 32))
                    largest(3, wr_f[:, :])
                if step == 5:
                    largest(2, wo_f, (s["w_in"], 16))
                for kc in {6: (0,), 7: (1,), 8: (2, 3)}.get(step, ()):
                    largest(4 + kc, wq_f[:, kc * 3 * D:(kc + 1) * 3 * D], (wq_in[kc], 16))

            def prepare():
                dve.wait_ge(s["const_in"], 16)
                nc.vector.tensor_copy(tid[:], conf[:, C_TOK:C_TOK + QB])
                nc.vector.tensor_copy(lt16[:], conf[:, C_LT:C_LT + P])
                nc.vector.memset(t1[:], 0.0).then_inc(s["largest"], 1)
                dve.wait_ge(s["largest"], 1)
                nc.vector.tensor_reduce(am[:, 0:1], am[:, 4:4 + KC], AX.X, ALU.max).then_inc(s["absmax"], 1)
                dve.wait_ge(s["allmax"], 1)
                setup(ts(amr[:, 0:4], amr[:, 0:4], 1e-9, None, ALU.max))
                setup(ts(amr[:, 1:2], amr[:, 0:1], float(D), amr[:, 1:2], ALU.mult, ALU.add))
                pow2(x(X_PA, 4), amr[:, 0:4])
                setup(nc.vector.reciprocal(x(X_SWQ, 4), x(X_PA, 4)))
                ts(x(X_SWQ, 4), x(X_SWQ, 4), 2.0 ** 14, None, ALU.mult).then_inc(s["scales"], 1)
                dve.wait_ge(s["scales"], 1)
                parts = list(weight_parts())

                def low_parts(n):
                    hi, lo, src, c = parts[n]
                    dve.wait_ge(s["w_split_hi"], n + 1)
                    nc.vector.scalar_tensor_tensor(out=lo, in0=src, scalar=x(c), in1=hi, op0=ALU.mult,
                                                   op1=ALU.subtract).then_inc(s["w_split_lo"], 1)

                setup(ts(x(X_T1), x(X_RPM), x(X_PA), None, ALU.mult))
                ts(x(X_CK), x(X_T1), 2.0 ** -24, None, ALU.mult)
                ts(x(X_CC), x(X_T1), 2.0 ** -20, None, ALU.mult)
                ts(x(X_CR), x(X_PAR), 2.0 ** -24, None, ALU.mult)
                ts(bqs[:], bqk[:], x(X_RPM), None, ALU.mult)
                setup(ts(cq[:], conf[:, C_F:C_F + NG], x(X_T1), None, ALU.mult))
                ts(cq[:], cq[:], 2.0 ** -30, None, ALU.mult)
                setup(nc.vector.tensor_tensor(bqs[:, 0:NG], bqs[:, 0:NG], conf[:, C_F:C_F + NG], ALU.mult))
                ts(bqs[:, 0:NG], bqs[:, 0:NG], 2.0 ** -6, None, ALU.mult).then_inc(s["biases"], 1)
                low_parts(0)
                ts(x(X_CS), x(X_PM), x(X_PAO), 2.0 ** -28, ALU.mult, ALU.mult)
                setup(ts(x(X_T0), x(X_PM), x(X_PM), 2.0 ** -22, ALU.mult, ALU.mult))
                setup(ts(nsl[:], conf[:, C_NSL:C_NSL + H], x(X_T0), None, ALU.mult))
                low_parts(1)
                setup(nc.vector.reciprocal(x(X_T0), x(X_T0)))
                setup(ts(base[:], conf[:, C_BASE:C_BASE + S], x(X_T0), None, ALU.mult))
                for n in range(2, len(parts)):
                    low_parts(n)
                dve.wait_ge(s["bout_in"], 16)

            LINKS = 17

            def iteration(b, odd):
                nxt, par = b + 1, 1 - odd
                more = within(b, -1, B - 1)
                k = [0]

                def link(ins):
                    k[0] += 1
                    ins.then_inc(s["dve_link"], 1)
                    wait(dve, s["dve_link"], (b + 1) * LINKS + k[0], s["apart_dve"])

                def ln_stats(i):
                    wait(dve, x_in[i], (nxt + 1) * 16)
                    link(nc.vector.bn_stats(stat[:, i, :], xin[:, i, :]))
                    nc.vector.bn_aggr(mv[:, i, :], stat[:, i, :]).then_inc(s["ln_stats"], 1)

                def ln_apply(i):
                    if i == 0:
                        wait(dve, s["rstd_ready"], nxt + 1)
                    wait(dve, s["xT_done"], b * QB + i + 1)
                    nc.vector.tensor_scalar(xn[:, i, :], xin[:, i, :], mv[:, i, 0:1], rstd[:, par, i:i + 1],
                                            ALU.subtract, ALU.mult).then_inc(s["xn_ready"], 1)

                def read_out(kind, bj, i, pj, ps):
                    if kind == "x":
                        wait(dve, s["xT_hi"], bj * QB + i + 1)
                        nc.vector.scalar_tensor_tensor(
                            out=xT[:, pj, 1, :, i * P:(i + 1) * P],
                            in0=ps[:].rearrange("p (k n) -> p k n", k=KC), scalar=1024.0,
                            in1=xT[:, pj, 0, :, i * P:(i + 1) * P], op0=ALU.mult, op1=ALU.subtract
                        ).then_inc(s["xT_lo"], 1)
                    elif kind == "v":
                        wait(dve, s["V_hi"], bj * QB + i + 1)
                        nc.vector.scalar_tensor_tensor(
                            out=v[:, pj, 1, i, :], in0=ps[:], scalar=2.0 ** -19,
                            in1=v[:, pj, 0, i, :], op0=ALU.mult, op1=ALU.subtract).then_inc(s["V_lo"], 1)
                    elif kind == "o":
                        wait(dve, s["O_done"], bj * QB + i + 2)
                        wait(dve, s_out[i], (bj + 1) * 16)
                        nc.vector.scalar_tensor_tensor(
                            out=so[:, i, :], in0=ps[:], scalar=x(X_CS),
                            in1=bout[:], op0=ALU.mult, op1=ALU.add).then_inc(s["O_evac"], 1)
                    elif kind == "logits":
                        choose(ps[:, 0:QB * E])
                    elif kind == "rank":
                        place(ps[:, 0:QB + 1])
                    else:
                        w, n = int(kind == "k"), (bj * NG + i) * 2
                        wait(dve, s["qk_staged"], n + 1 + w)
                        wait(dve, stored[w], (bj * NG + i) * 16)
                        nc.vector.tensor_copy(pre[:, w, 0, :], stage[:, w, :]).then_inc(s["qk_hi"], 1)

                def choose(psR):
                    wait(dve, s["R_done"], nxt + 1)
                    wait(dve, s["R2_done"], nxt)
                    ts(lg[:].rearrange("p i e -> p (i e)"), psR, x(X_CR), None, ALU.mult
                       ).then_inc(s["logits_read"], 1)
                    dve.wait_ge(s["logits_read"], nxt + 1)
                    link(nc.vector.tensor_tensor(dl[:], lg[:, :, 1], lg[:, :, 0], ALU.subtract))
                    nc.vector.scalar_tensor_tensor(out=nd[:], in0=dl[:], scalar=-1.0, in1=dl[:],
                                                   op0=ALU.mult, op1=ALU.min).then_inc(s["nd_ready"], 1)
                    link(ts(ef[:, 0:QB], dl[:], 0.0, None, ALU.is_gt))
                    nc.vector.tensor_copy(e16[:, 0:QB], ef[:, 0:QB])
                    link(nc.vector.tensor_copy(epre[:, 1:2], ef[:, 0:1]))
                    for i in range(1, QB):
                        link(nc.vector.tensor_tensor(epre[:, i + 1:i + 2], epre[:, i:i + 1], ef[:, i:i + 1],
                                                     ALU.add))
                    nc.vector.memset(t0[:, 0:1], 0.0).then_inc(s["e_ready"], 1)

                def place(psK):
                    wait(dve, s["R2_done"], nxt + 1)
                    wait(dve, s["rexp_done"], nxt + 1)
                    wait(dve, s["meta_out"], nxt * QB * 16)
                    nc.vector.tensor_scalar(rk[:], psK, esum[:, 0:1], None, ALU.add
                                            ).then_inc(s["rank_read"], 1)
                    dve.wait_ge(s["rank_read"], nxt + 1)
                    nc.vector.tensor_copy(esum[:, 0:1], rk[:, QB:QB + 1])
                    link(nc.vector.tensor_tensor(t0[:], tid[:], rk[:, 0:QB], ALU.subtract))
                    link(ts(t1[:], tid[:], -1.0, float(TOK - 1), ALU.mult, ALU.add))
                    link(nc.vector.tensor_tensor(t1[:], t1[:], ef[:, 0:QB], ALU.mult))
                    link(nc.vector.tensor_tensor(t0[:], t0[:], t1[:], ALU.add))
                    nc.vector.tensor_copy(pos[:], t0[:])
                    nc.vector.tensor_copy(meta[:, :, 0], tid[:])
                    link(ts(t1[:], ex[:], 1.0, None, ALU.add))
                    nc.vector.tensor_copy(meta[:, :, 2], ef[:, 0:QB])
                    nc.vector.tensor_copy(meta[:, :, 3], mv[:, :, 0])
                    nc.vector.tensor_copy(meta[:, :, 4], rstd[:, par, :])
                    link(nc.vector.reciprocal(meta[:, :, 1], t1[:]))
                    link(ts(tid[:], tid[:], float(S), None, ALU.add))
                    nc.vector.memset(rk[:, 0:1], 0.0).then_inc(s["meta_ready"], 1)

                for step in range(H):
                    g, j = step // HG, step % HG
                    if isinstance(b, int) and b == -1:
                        magnitudes(step)
                        if step == 8:
                            prepare()
                    hd = b * H + step
                    hb, h = head_at(b, step + M_LEAD)

                    def low(r):
                        if not within(b, 0, B):
                            return
                        kbs = TJOBS[r]
                        w = sum(S - kb * P for kb in kbs)
                        o = SEG[kbs[0]]
                        wait(dve, s["T_hi"], hd * 3 + r + 1)
                        nc.vector.tensor_tensor(pt[:, g % 2, 1, j, o:o + w], psT[r][:, 0:w],
                                                pt[:, g % 2, 0, j, o:o + w], ALU.subtract
                                                ).then_inc(s["T_lo"], 1)

                    def masked(i):
                        if not within(hb, 0, B):
                            return
                        if i == 0:
                            wait(dve, s["T_done"], (hb * H + h - HG + 1) * 3)
                        w = (i + 1) * P
                        c = (h % HG) * QB + i
                        wait(dve, s["S_done"], (hb * H + h) * QB + max(i, 1) + 1, s["apart_dve"])
                        nc.vector.tensor_tensor_reduce(
                            out=pr[:, h % HG, ROWOFF[i]:ROWOFF[i] + w], in0=rows[i],
                            in1=base[:, S - w:S], scale=nsl[:, h:h + 1], scalar=3e38,
                            op0=ALU.add, op1=ALU.min, accum_out=mn[:, c:c + 1]).then_inc(s["ttr_done"], 1)

                    rb, rh = head_at(b, step + N_LEAD)
                    if within(rb, 0, B):
                        wait(dve, s["exp_done"], (rb * H + rh + 1) * QB)
                        wait(dve, s["norm_done"], (rb * H + rh - HG + 1) * QB)
                        c = (rh % HG) * QB
                        nc.vector.reciprocal(rden[:, c:c + QB], den[:, c:c + QB]).then_inc(s["rden_done"], 1)
                    masked(0)
                    masked(1)
                    masked(2)
                    masked(3)
                    low(0)
                    low(1)
                    for args in jobs(b, odd, step):
                        read_out(*args)
                    low(2)
                    if more:
                        if step < 2:
                            ln_stats(2 * step)
                            ln_stats(2 * step + 1)
                        elif step < 6:
                            ln_apply(step - 2)
                    if within(b, 0, B) and step in WMAX_AT:
                        m = WMAX_AT.index(step)
                        c, lo = m // 2, m % 2 * (2048 // 2)
                        wait(dve, s["wmax_in"], (b * 2 + c + 1) * 16)
                        nc.vector.tensor_reduce(fam[:, 2:3], wst[:, lo:lo + 2048 // 2], AX.X, ALU.max,
                                                apply_absolute_value=True).then_inc(s["wmax_done"], 1)
                        dve.wait_ge(s["wmax_done"], b * 4 + m + 1)
                        nc.vector.tensor_tensor(fam[:, c:c + 1], fam[:, c:c + 1], fam[:, 2:3], ALU.max
                                                ).then_inc(s["wm_link"], 1)
                        dve.wait_ge(s["wm_link"], b * 4 + m + 1)
                    if j == (3 if g else 2):
                        pb, pg = (b, g - 1) if g else (b - 1, NG - 1)
                        if within(pb, 0, B):
                            wait(dve, s["ctx_staged"], pb * NG + pg + 1)
                            wait(dve, s["O_done"], pb * QB + 1)
                            nc.vector.tensor_copy(cx[:, pg, 0, :], cf[:]).then_inc(s["ctx_hi"], 1)
                assert not more or k[0] == LINKS, k[0]

            batches(dve, iteration)
            dve.wait_ge(s["allmax"], 2)
            setup(ts(x(X_PA1, 2), x(X_PA1, 2), 1e-9, None, ALU.max))
            setup(ts(x(X_PA1, 2).bitcast(I32), x(X_PA1, 2).bitcast(I32), 0x7F800000, None, ALU.bitwise_and))
            setup(nc.vector.reciprocal(x(X_S1, 2), x(X_PA1, 2)))
            setup(ts(x(X_S1, 2), x(X_S1, 2), 2.0 ** 14, None, ALU.mult))
            setup(nc.vector.tensor_tensor(x(X_CY), x(X_PA1), x(X_PA1), ALU.mult))
            setup(nc.vector.tensor_tensor(x(X_CY), x(X_CY), x(X_PA2), ALU.mult))
            setup(ts(x(X_CY), x(X_CY), 2.0 ** -8, None, ALU.mult))
            setup(ts(n0[:], esum[:, 0:1], -1.0, float(TOK), ALU.mult, ALU.add))
            setup(ts(n0[:], n0[:], float(TOK - 1), None, ALU.min))
            setup(ts(eslot[:], conf[:, C_SLOT:C_SLOT + SLOTS], n0[:, 0:1], None, ALU.is_gt))
            setup(nc.vector.tensor_copy(eint[:], eslot[:]))
            setup(nc.vector.scalar_tensor_tensor(out=tint[:], in0=conf[:, C_SLOT:C_SLOT + SLOTS], scalar=1.0 / P,
                                                in1=eslot[:], op0=ALU.mult, op1=ALU.subtract))

        @block.gpsimd
        def _(pool):
            def iteration(b, odd):
                nxt, par = b + 1, 1 - odd
                more = within(b, -1, B - 1)
                for step in range(H):
                    g, j = step // HG, step % HG
                    if isinstance(b, int) and b == -1 and step == 8:
                        pool.wait_ge(s["absmax"], 1)
                        nc.gpsimd.partition_all_reduce(amr[:, 0:4], am[:, 0:4], P, RMAX
                                                       ).then_inc(s["allmax"], 1)
                    rb, rh = head_at(b, step + N_LEAD)
                    if within(rb, 0, B):
                        wait(pool, s["rden_done"], rb * H + rh + 1, s["apart_pool"])
                        for i in range(QB):
                            c = (rh % HG) * QB + i
                            p_ = pr[:, rh % HG, ROWOFF[i]:ROWOFF[i] + (i + 1) * P]
                            nc.gpsimd.tensor_scalar(p_, p_, rden[:, c:c + 1], 32768.0, ALU.mult, ALU.mult
                                                    ).then_inc(s["norm_done"], 1)
                    for kind, bj, i, _, _ in jobs(b, odd, step, ("q", "k")):
                        w = int(kind == "k")
                        wait(pool, s["qk_hi"], (bj * NG + i) * 2 + 1 + w, s["apart_pool"])
                        nc.gpsimd.tensor_tensor(pre[:, w, 1, :], stage[:, w, :], pre[:, w, 0, :],
                                                ALU.subtract).then_inc(s["qk_lo"], 1)
                    if more and step == 1:
                        wait(pool, s["ln_stats"], (nxt + 1) * QB, s["apart_pool"])
                        wait(pool, s["meta_ready"], nxt - 1, s["apart_pool"])
                        nc.gpsimd.tensor_scalar(veps[:], mv[:, :, 1], 1e-5, 1.0, ALU.add, ALU.mult
                                                ).then_inc(s["pool_link"], 1)
                        wait(pool, s["pool_link"], nxt + 1, s["apart_pool"])
                        nc.gpsimd.tensor_tensor(rstd[:, par, :], veps[:], half[:], ALU.pow
                                                ).then_inc(s["rstd_ready"], 1)
                    pb, pg = (b, g - 1) if g else (b - 1, NG - 1)
                    if j == (3 if g else 2) and within(pb, 0, B):
                        wait(pool, s["ctx_hi"], pb * NG + pg + 1, s["apart_pool"])
                        nc.gpsimd.tensor_tensor(cx[:, pg, 1, :], cf[:], cx[:, pg, 0, :], ALU.subtract
                                                ).then_inc(s["ctx_lo"], 1)
                    if more and step in (14, 15):
                        wait(pool, s["meta_ready"], nxt + 1, s["apart_pool"])
                        for i in (2 * step - 28, 2 * step - 27):
                            nc.gpsimd.indirect_dma_start(
                                out=io["meta"], out_offset=bass.IndirectOffsetOnAxis(ap=pos[:, i:i + 1], axis=0),
                                in_=meta[:, i, :], in_offset=None).then_inc(s["meta_out"], 16)

            batches(pool, iteration)
            pool.wait_ge(s["meta_out"], 16 * QB * B)
            pool.wait_ge(s["wm_link"], 4 * B)
            nc.gpsimd.partition_all_reduce(sc[:, X_PA1:X_PA1 + 2], fam[:, 0:2], P, RMAX
                                           ).then_inc(s["allmax"], 1)
            pool.wait_ge(s["allmax"], 2)


def ffn_block(nc, io, sc, conf, mall, eslot, eint, tint):
    with ExitStack() as ctx:
        sb = lambda n, s, d: ctx.enter_context(nc.sbuf_tensor(n, s, d))
        sem = lambda n: ctx.enter_context(nc.semaphore(n))
        NP = 2 * HC
        HP, RING = 1024, 5
        wf = sb("wf", [P, E, NP, 2, 2048], F16)
        wstage = sb("wstage", [P, RING, HP], F32)
        rec = sb("rec", [P, 4, MROW], F32)
        gidx = sb("gidx", [P, 4], I32)
        oidx = sb("oidx", [P, 2], I32)
        miss = sb("miss", [P, 1], F32)
        xg = sb("xg", [P, 4, D], F32)
        sg = sb("sg", [P, 2, D], F32)
        xn = sb("xn2", [P, D], F32)
        xT = sb("xT2", [P, 2, 2, D], F16)
        rl = sb("rl", [P, 2, 512], F32)
        a = sb("a", [P, 2, HC, 512], F32)
        aT = sb("aT", [P, 2, 2, 512], F16)
        z = sb("z", [P, D], F32)
        gt = sb("gt", [P, D], F32)
        ob = sb("ob", [P, D], F32)
        psF = [ctx.enter_context(nc.psum_tensor(f"psF{i}", [P, 512], F32)) for i in range(2)]
        psT = [ctx.enter_context(nc.psum_tensor(f"psU{i}", [P, 512], F32)) for i in range(2)]
        psX = ctx.enter_context(nc.psum_tensor("psX", [P, 512], F32))
        psY = [ctx.enter_context(nc.psum_tensor(f"psY{i}", [P, 512], F32)) for i in range(2)]
        names = ("ws_hi ws_lo idx_ready ln_done X_done X_hi X_lo F_done f_relu f_sum "
                 "a_ready U_done U_hi U_lo Y_done z_ready g_exp o_ready ob_free apart_pool f_link out_done").split()
        s = {n: sem("f_" + n) for n in names}
        w_in = [sem(f"wf_in{i}") for i in range(RING)]
        x_got = [sem(f"x_got{i}") for i in range(4)]
        s_got = [sem(f"s_got{i}") for i in range(2)]
        block = ctx.enter_context(nc.Block())
        LOOPS = (SLOTS - 4) // 4

        def arrived(n, r, ring):
            return (n - (r % ring) + ring) * (16 // ring)

        def slots(eng, step):
            for n in range(-3, 1):
                step(n, n % 4)
            with eng.Fori(0, LOOPS) as it:
                for q in range(4):
                    step(it * 4 + (q + 1), (q + 1) % 4)
            for n in range(4 * LOOPS + 1, SLOTS + 1):
                step(n, n % 4)

        @block.sync
        def _(sp):
            for n in range(E * NP * 2):
                if n >= RING:
                    sp.wait_ge(s["ws_lo"], n - RING + 1)
                c = n % 2 * HP
                sp.dma_start(wstage[:, n % RING, :], io["wf"][n // 2, :, c:c + HP]).then_inc(w_in[n % RING], 16)

        @block.tensor
        def _(pe):
            def expert(eng_s):
                return pe.value_load(eint[0:1, bass.ds(eng_s, 1)], min_val=0, max_val=1)

            def w(e, piece, hl, c):
                return wf[:, bass.ds(e, 1), piece, hl, c * 512:(c + 1) * 512].rearrange("p o n -> p (o n)")

            def xtrans(n, r):
                wait(pe, s["ln_done"], n + 1)
                wait(pe, s["X_lo"], n)
                for kc in range(KC):
                    last = nc.tensor.transpose(psX[:, kc * P:(kc + 1) * P], xn[:, kc * P:(kc + 1) * P],
                                               conf[:, C_ID:C_ID + P])
                last.then_inc(s["X_done"], 1)

            def up(n, r, hc, e):
                t = n * HC + hc
                if hc == 0:
                    wait(pe, s["X_lo"], n + 1)
                if isinstance(n, int):
                    wait(pe, s["ws_lo"], 2 * (2 * hc + 1 + (NP if n > 0 else 0)))
                ps = psF[hc % 2]
                wait(pe, s["f_sum"], t - 1)
                k = 0
                for x, hl in ((0, 0), (1, 0), (0, 1)):
                    for kc in range(KC):
                        last = nc.tensor.matmul(ps[:], xT[:, r % 2, x, kc * P:(kc + 1) * P],
                                                w(e, 2 * hc, hl, kc), start=(k == 0), stop=(k == 3 * KC - 1))
                        k += 1
                last.then_inc(s["F_done"], 1)

            def turn(n, r, hc):
                t = n * HC + hc
                wait(pe, s["a_ready"], t + 1)
                wait(pe, s["U_lo"], t - 1)
                for q in range(4):
                    last = nc.tensor.transpose(psT[hc % 2][:, q * P:(q + 1) * P],
                                               a[:, r % 2, hc, q * P:(q + 1) * P], conf[:, C_ID:C_ID + P])
                last.then_inc(s["U_done"], 1)

            def down(n, r, hc, e):
                t = n * HC + hc
                if hc == 0:
                    wait(pe, s["z_ready"], n)
                if isinstance(n, int):
                    wait(pe, s["ws_lo"], 2 * (2 * hc + 2 + (NP if n > 0 else 0)))
                wait(pe, s["U_lo"], t + 1)
                k = 0
                for x, hl in ((0, 0), (1, 0), (0, 1)):
                    for q in range(4):
                        last = nc.tensor.matmul(psY[r % 2][:], aT[:, hc % 2, x, q * P:(q + 1) * P],
                                                w(e, 2 * hc + 1, hl, q), start=(hc == 0 and k == 0),
                                                stop=(hc == HC - 1 and k == 11))
                        k += 1
                last.then_inc(s["Y_done"], 1)

            def step(n, r):
                here, ahead = within(n, 0, SLOTS), within(n + 1, 0, SLOTS)
                e0 = expert(n) if here else None
                e1 = expert(n + 1) if ahead else None
                if ahead and not isinstance(n, int):
                    pe.wait_ge(s["ws_lo"], E * NP * 2)
                for hc in range(HC):
                    if here:
                        turn(n, r, hc)
                    if here and hc > 0:
                        down(n, r, hc - 1, e0)
                    if ahead:
                        up(n + 1, r + 1, hc, e1)
                    if hc == 1 and within(n + 2, 0, SLOTS):
                        xtrans(n + 2, r + 2)
                if here:
                    down(n, r, HC - 1, e0)

            slots(pe, step)

        @block.scalar
        def _(act):
            def split(m):
                for n in range(m * 4, (m + 1) * 4 if m < E * HC else 0):
                    e, q, h = n // (2 * NP), n // 2 % NP, n % 2 * HP
                    act.wait_ge(w_in[n % RING], (n // RING + 1) * 16)
                    c = X_S1 + q % 2
                    nc.scalar.activation(wf[:, e, q, 0, h:h + HP], wstage[:, n % RING, :], ACT.Copy,
                                         scale=sc[:, c:c + 1]).then_inc(s["ws_hi"], 1)

            def relu(n, r, hc):
                t = n * HC + hc
                wait(act, s["F_done"], t + 1)
                wait(act, s["f_sum"], t - 1)
                nc.scalar.activation(rl[:, hc % 2, :], psF[hc % 2][:], ACT.Relu, scale=2.0 ** -28
                                     ).then_inc(s["f_relu"], 1)

            def uhi(n, r, hc):
                t = n * HC + hc
                wait(act, s["U_done"], t + 1)
                wait(act, s["Y_done"], t - 1)
                nc.scalar.activation(aT[:, hc % 2, 0, :], psT[hc % 2][:], ACT.Copy).then_inc(s["U_hi"], 1)

            def step(n, r):
                here, ahead = within(n, 0, SLOTS), within(n + 1, 0, SLOTS)
                if isinstance(n, int) and n == -3:
                    split(0)
                for hc in range(HC):
                    if here:
                        uhi(n, r, hc)
                    if isinstance(n, int) and n in (-1, 0):
                        split((n + 1) * HC + hc + 1)
                    if ahead:
                        relu(n + 1, r + 1, hc)
                    if hc == 1 and within(n - 1, 0, SLOTS):
                        wait(act, s["z_ready"], n + 1)
                        nc.scalar.activation(gt[:], gt[:], ACT.Exp, scale=-1.0).then_inc(s["g_exp"], 1)
                    if hc == 1 and within(n + 2, 0, SLOTS):
                        wait(act, s["X_done"], n + 3)
                        wait(act, s["F_done"], (n + 1) * HC)
                        nc.scalar.activation(xT[:, r % 2, 0, :], psX[:], ACT.Copy, scale=1024.0
                                             ).then_inc(s["X_hi"], 1)

            slots(act, step)

        @block.vector
        def _(dve):
            ts = nc.vector.tensor_scalar
            x = lambda c, n=1: sc[:, c:c + n]
            nc.vector.memset(ob[:, 0:1], 0.0).then_inc(s["z_ready"], 1)
            LK = 7

            def split(m):
                for n in range(m * 4, (m + 1) * 4 if m < E * HC else 0):
                    e, q, h = n // (2 * NP), n // 2 % NP, n % 2 * HP
                    dve.wait_ge(s["ws_hi"], n + 1)
                    c = X_S1 + q % 2
                    nc.vector.scalar_tensor_tensor(out=wf[:, e, q, 1, h:h + HP], in0=wstage[:, n % RING, :],
                                                   scalar=sc[:, c:c + 1], in1=wf[:, e, q, 0, h:h + HP],
                                                   op0=ALU.mult, op1=ALU.subtract).then_inc(s["ws_lo"], 1)

            def fetch(n, r):
                tile = dve.value_load(tint[0:1, bass.ds(n, 1)], min_val=0, max_val=TOK // P - 1)
                src = mall[:, bass.ds(tile, 1), :].rearrange("p o c -> p (o c)")
                nc.vector.tensor_copy(rec[:, r % 4, :], src)
                nc.vector.tensor_copy(gidx[:, r % 4:r % 4 + 1], src[:, 0:1]).then_inc(s["idx_ready"], 1)

            def total(n, r, hc):
                t = n * HC + hc
                wait(dve, s["f_relu"], t + 1)
                wait(dve, s["U_done"], t - 2 * HC + 1)
                nc.vector.scalar_tensor_tensor(out=a[:, r % 2, hc, :], in0=psF[hc % 2][:], scalar=2.0 ** -28,
                                               in1=rl[:, hc % 2, :], op0=ALU.mult, op1=ALU.add
                                               ).then_inc(s["f_sum"], 1)

            def ulo(n, r, hc):
                t = n * HC + hc
                wait(dve, s["U_hi"], t + 1)
                nc.vector.tensor_tensor(aT[:, hc % 2, 1, :], psT[hc % 2][:], aT[:, hc % 2, 0, :], ALU.subtract
                                        ).then_inc(s["U_lo"], 1)

            def step(n, r):
                here, ahead = within(n, 0, SLOTS), within(n + 1, 0, SLOTS)
                done = within(n - 1, 0, SLOTS)
                k = [0]

                def link(ins):
                    k[0] += 1
                    ins.then_inc(s["f_link"], 1)
                    dve.wait_ge(s["f_link"], (n - 1) * LK + k[0])

                if done:
                    m = n - 1
                    rm = (r - 1) % 4
                    wait(dve, s["Y_done"], n * HC)
                    link(ts(z[:], psY[rm % 2][:], rec[:, rm, 1:2], x(X_CY), ALU.mult, ALU.mult))
                    nc.vector.tensor_scalar(gt[:], z[:], -80.0, None, ALU.max).then_inc(s["z_ready"], 1)
                for hc in range(HC):
                    if here:
                        ulo(n, r, hc)
                    if isinstance(n, int) and n in (-1, 0):
                        split((n + 1) * HC + hc + 1)
                    if ahead:
                        total(n + 1, r + 1, hc)
                    if done and hc == 1:
                        wait(dve, s["g_exp"], n)
                        link(ts(gt[:], gt[:], 1.0, None, ALU.add))
                        link(nc.vector.reciprocal(gt[:], gt[:]))
                    if done and hc == 2:
                        wait(dve, s_got[rm % 2], arrived(n - 1, rm, 2))
                        wait(dve, s["ob_free"], n)
                        link(nc.vector.tensor_tensor(z[:], z[:], gt[:], ALU.mult))
                        link(nc.vector.tensor_tensor(z[:], z[:], sg[:, rm % 2, :], ALU.mult))
                        link(ts(miss[:], rec[:, rm, 2:3], esl(n - 1), float(OOB), ALU.not_equal, ALU.mult))
                        link(nc.vector.tensor_tensor(oidx[:, rm % 2:rm % 2 + 1], miss[:], rec[:, rm, 0:1],
                                                     ALU.add))
                        nc.vector.tensor_tensor(ob[:], z[:], xg[:, rm, :], ALU.add).then_inc(s["o_ready"], 1)
                        dve.wait_ge(s["o_ready"], n)
                    if hc == 2 and within(n + 3, 0, SLOTS):
                        fetch(n + 3, r + 3)
                    if hc == 0 and within(n + 2, 0, SLOTS):
                        r2 = (r + 2) % 4
                        wait(dve, x_got[r2], arrived(n + 2, r2, 4))
                        wait(dve, s["X_done"], n + 2)
                        dve.wait_ge(s["idx_ready"], n + 3)
                        nc.vector.tensor_scalar(xn[:], xg[:, r2, :], rec[:, r2, 3:4], rec[:, r2, 4:5],
                                                ALU.subtract, ALU.mult).then_inc(s["ln_done"], 1)
                    if hc == 1 and within(n + 2, 0, SLOTS):
                        wait(dve, s["X_hi"], n + 3)
                        nc.vector.scalar_tensor_tensor(out=xT[:, r % 2, 1, :], in0=psX[:], scalar=1024.0,
                                                       in1=xT[:, r % 2, 0, :], op0=ALU.mult, op1=ALU.subtract
                                                       ).then_inc(s["X_lo"], 1)
                if isinstance(n, int) and n == -3:
                    split(0)
                assert not done or k[0] == LK

            def esl(n):
                return eslot[:, bass.ds(n, 1)]

            slots(dve, step)

        @block.gpsimd
        def _(pool):
            def gather(dst, src, r, sm):
                nc.gpsimd.indirect_dma_start(out=dst, out_offset=None, in_=src,
                                             in_offset=bass.IndirectOffsetOnAxis(ap=gidx[:, r % 4:r % 4 + 1], axis=0)
                                             ).then_inc(sm, 16)

            def step(n, r):
                done = within(n - 1, 0, SLOTS)
                for hc in range(HC):
                    if within(n + 1, 0, SLOTS):
                        t = (n + 1) * HC + hc
                        wait(pool, s["f_sum"], t + 1, s["apart_pool"])
                        at = a[:, (r + 1) % 2, hc, :]
                        nc.gpsimd.tensor_tensor(at, at, at, ALU.mult).then_inc(s["a_ready"], 1)
                    if hc == 2 and done:
                        wait(pool, s["o_ready"], n, s["apart_pool"])
                        rm = (r - 1) % 4
                        nc.gpsimd.indirect_dma_start(
                            out=io["out"],
                            out_offset=bass.IndirectOffsetOnAxis(ap=oidx[:, rm % 2:rm % 2 + 1], axis=0),
                            in_=ob[:], in_offset=None, bounds_check=TOK - 1, oob_is_err=False
                        ).then_inc(s["out_done"], 16)
                    if hc == 2 and within(n + 3, 0, SLOTS):
                        wait(pool, s["idx_ready"], n + 4, s["apart_pool"])
                        gather(xg[:, (r + 3) % 4, :], io["x"], r + 3, x_got[(r + 3) % 4])
                    if hc == 2 and within(n + 1, 0, SLOTS):
                        gather(sg[:, (r + 1) % 2, :], io["s"], r + 1, s_got[(r + 1) % 2])
                if done:
                    wait(pool, s["out_done"], n * 16, s["apart_pool"])
                    pool.sem_inc(s["ob_free"], 1)

            pool.sem_inc(s["ob_free"], 1)
            slots(pool, step)
            pool.wait_ge(s["out_done"], SLOTS * 16)


def build(nc, x, wqkv, bqkv, wout, bout, wr, wf, const, out):
    io = {"x": x, "wqkv": wqkv, "bqkv": bqkv, "wout": wout, "bout": bout, "wr": wr, "wf": wf,
          "const": const, "out": out,
          "s": nc.dram_tensor("attn_out", [TOK, D], F32).ap(),
          "meta": nc.dram_tensor("route", [TOK, MROW], F32).ap(),
          "qk": nc.dram_tensor("qk_parts", [2, 2, 2, P, S], F16).ap()}
    with ExitStack() as ctx:
        sc = ctx.enter_context(nc.sbuf_tensor("sc", [P, X_N], F32))
        conf = ctx.enter_context(nc.sbuf_tensor("conf", [P, C_N], F32))
        esum = ctx.enter_context(nc.sbuf_tensor("esum", [P, 1], F32))
        mall = ctx.enter_context(nc.sbuf_tensor("mall", [P, TOK // P, MROW], F32))
        eslot = ctx.enter_context(nc.sbuf_tensor("eslot", [P, SLOTS], F32))
        eint = ctx.enter_context(nc.sbuf_tensor("eint", [P, SLOTS], I32))
        tint = ctx.enter_context(nc.sbuf_tensor("tint", [P, SLOTS], I32))
        attention_block(nc, io, sc, conf, esum, mall, eslot, eint, tint)
        ffn_block(nc, io, sc, conf, mall, eslot, eint, tint)


def kernel(L0_attn_x, L0_attn_Wqkv, L0_attn_b_qkv, L0_attn_Wout, L0_attn_b_out,
           L0_ffn_w_router, L0_ffn_w_fc, L0_ffn_w_proj):
    import concourse.bacc as bacc
    from concourse.bass_utils import run_bass_kernel_spmd

    def lhs(w, k):
        w = np.asarray(w)
        return np.ascontiguousarray(w.T.reshape(k, P, -1).transpose(1, 0, 2).reshape(P, -1))

    w1 = np.asarray(L0_ffn_w_fc).reshape(E, HC, 512, KC, P).transpose(0, 1, 4, 3, 2).reshape(E, HC, P, 2048)
    w2 = np.asarray(L0_ffn_w_proj).reshape(E, D, HC, 4, P).transpose(0, 2, 4, 3, 1).reshape(E, HC, P, 2048)
    arrays = {
        "x": np.ascontiguousarray(np.asarray(L0_attn_x).reshape(TOK, D)),
        "wqkv": lhs(L0_attn_Wqkv, KC),
        "bqkv": np.ascontiguousarray(np.asarray(L0_attn_b_qkv).reshape(3 * NG, P).T),
        "wout": lhs(L0_attn_Wout, NG),
        "bout": np.ascontiguousarray(np.broadcast_to(np.asarray(L0_attn_b_out), (P, D))),
        "wr": lhs(L0_ffn_w_router, KC),
        "wf": np.ascontiguousarray(np.stack([w1, w2], 2).reshape(E * HC * 2, P, 2048)),
        "const": constants(),
    }
    nc = bacc.Bacc("TRN2", target_bir_lowering=False, num_devices=1)
    args = [nc.dram_tensor("in_" + n, a.shape, mybir.dt.from_np(a.dtype), kind="ExternalInput").ap()
            for n, a in arrays.items()]
    args.append(nc.dram_tensor("out_x", (TOK, D), F32, kind="ExternalOutput").ap())
    build(nc, *args)
    r = run_bass_kernel_spmd(nc, [{"in_" + n: a for n, a in arrays.items()}], core_ids=[0])
    return r.results[0]["out_x"].reshape(B, S, D)
```
